# Optimizing a Trainium2 kernel written in Bass

```python
import numpy as np
import jax
import jax.numpy as jnp

def _softmax(x, axis=-1):
    return jax.nn.softmax(x, axis=axis)

def _gelu(x):
    return jax.nn.gelu(x, approximate=True)

def _silu(x):
    return jax.nn.silu(x)

def _sigmoid(x):
    return jax.nn.sigmoid(x)

def _layernorm(x, axis=-1, eps=1e-05):
    m = jnp.mean(x, axis=axis, keepdims=True)
    v = jnp.var(x, axis=axis, keepdims=True)
    return (x - m) / jnp.sqrt(v + eps)

def _scatter_add(tgt, idx, src, axis=0):
    return tgt.at[idx].add(src)

def _segment_sum(src, seg, n):
    return jax.ops.segment_sum(src, seg, n)
kernel_name = 'mk_gnn_preln_d4_gnn_r32_ae6f91'

def setup_inputs(seed: int=0):
    np.random.seed(seed)
    _w = jnp.asarray

    def _rec_inputs():
        import jax
        import jax.numpy as jnp
        _gk = jax.random.key(seed)
        x = -0.0005963 + 1.001 * jax.random.normal(jax.random.fold_in(_gk, 1), (96, 1024), jnp.float32)
        src = jax.random.randint(jax.random.fold_in(_gk, 2), (1536,), 0, 96, jnp.int32)
        dst = jax.random.randint(jax.random.fold_in(_gk, 3), (1536,), 0, 96, jnp.int32)
        _o = jnp.argsort(dst, stable=True)
        src = src[_o]
        dst = dst[_o]
        edge_type_5 = jax.random.randint(jax.random.fold_in(_gk, 12), (1536,), 0, 5, jnp.int32)
        edge_weight = -0.000130211 + 0.031236 * jax.random.normal(jax.random.fold_in(_gk, 13), (1536,), jnp.float32)
        return (x, src, dst, edge_type_5, edge_weight)
    x, src, dst, edge_type_5, edge_weight = _rec_inputs()

    def _L0_gnn_setup():
        import jax, jax.numpy as jnp
        import numpy as np
        N = 96
        E = 3072
        IN_F = 1024
        OUT_F = 1024
        H = 16
        D = OUT_F // H
        NUM_ETYPES = 4

        def _build_mask(edge_index, edge_type, edge_type_weights, dtype):
            src, dst = (edge_index[0], edge_index[1])
            w = jax.nn.softplus(edge_type_weights)
            mask = jnp.full((N, N), -jnp.inf, dtype=dtype)
            mask = mask.at[src, dst].set(w[edge_type - 1])
            diag = jnp.diagonal(mask)
            idx = jnp.arange(N)
            mask = mask.at[idx, idx].set(jnp.where(jnp.isneginf(diag), w[3], diag))
            return mask
        key = jax.random.key(seed)
        ks = jax.random.split(key, 20)
        p = lambda k, shape: jax.random.normal(k, shape, dtype=jnp.float32) * 0.02
        return {'x': jax.random.normal(ks[0], (N, IN_F), dtype=jnp.float32), 'edge_index': jax.random.randint(ks[1], (2, E), 0, N), 'edge_type': jax.random.randint(ks[2], (E,), 1, NUM_ETYPES + 1), 'edge_type_weights': jnp.ones((NUM_ETYPES,), jnp.float32) + 0.1 * jax.random.normal(ks[3], (NUM_ETYPES,), dtype=jnp.float32), 'wq': p(ks[4], (OUT_F, IN_F)), 'bq': p(ks[5], (OUT_F,)), 'wk': p(ks[6], (OUT_F, IN_F)), 'bk': p(ks[7], (OUT_F,)), 'wv': p(ks[8], (OUT_F, IN_F)), 'bv': p(ks[9], (OUT_F,)), 'wiq': p(ks[10], (OUT_F, OUT_F)), 'biq': p(ks[11], (OUT_F,)), 'wik': p(ks[12], (OUT_F, OUT_F)), 'bik': p(ks[13], (OUT_F,)), 'wiv': p(ks[14], (OUT_F, OUT_F)), 'biv': p(ks[15], (OUT_F,)), 'wo': p(ks[16], (OUT_F, OUT_F)), 'bo': p(ks[17], (OUT_F,))}
    _L0_gnn_all = _L0_gnn_setup()
    _L0_gnn_in = {k: v for k, v in _L0_gnn_all.items() if k in ('edge_type_weights', 'wq', 'bq', 'wk', 'bk', 'wv', 'bv', 'wiq', 'biq', 'wik', 'bik', 'wiv', 'biv', 'wo', 'bo')}
    del _L0_gnn_all

    def _L1_gnn_setup():
        import jax, jax.numpy as jnp
        import numpy as np
        INDIM = 1024
        OUTDIM = 1024
        NNZ = 2048
        N = 50000
        key = jax.random.key(seed)
        k1, k2, k3, k4, k5 = jax.random.split(key, 5)
        x = jax.random.normal(k1, (N, INDIM), dtype=jnp.float32)
        stdv = np.sqrt(6.0 / (INDIM + OUTDIM))
        nnz_weight = jax.random.uniform(k2, (NNZ,), dtype=jnp.float32, minval=-stdv, maxval=stdv)
        bias = jax.random.normal(k3, (OUTDIM,), dtype=jnp.float32) * 0.02
        row = jax.random.randint(k4, (NNZ,), 0, OUTDIM, dtype=jnp.int64)
        col = jax.random.randint(k5, (NNZ,), 0, INDIM, dtype=jnp.int64)
        edge_index = jnp.stack([row, col])
        return {'x': x, 'nnz_weight': nnz_weight, 'bias': bias, 'edge_index': edge_index}
    _L1_gnn_all = _L1_gnn_setup()
    _L1_gnn_in = {k: v for k, v in _L1_gnn_all.items() if k in ('bias',)}
    del _L1_gnn_all

    def _L2_gnn_setup():
        import jax, jax.numpy as jnp
        import numpy as np
        N = 625
        E = 10000
        D_IN = 1024
        D_OUT = 1024
        key = jax.random.key(seed)
        k1, k2, k3, k4 = jax.random.split(key, 4)
        x = jax.random.normal(k1, (N, D_IN), dtype=jnp.float32)
        edge_index = jax.random.randint(k2, (2, E), 0, N, dtype=jnp.int64)
        W = jax.random.normal(k3, (D_OUT, D_IN), dtype=jnp.float32) * (1.0 / np.sqrt(D_IN))
        b = jax.random.normal(k4, (D_OUT,), dtype=jnp.float32) * 0.01
        return {'x': x, 'edge_index': edge_index, 'W': W, 'b': b}
    _L2_gnn_all = _L2_gnn_setup()
    _L2_gnn_in = {k: v for k, v in _L2_gnn_all.items() if k in ('W', 'b')}
    del _L2_gnn_all

    def _L3_gnn_setup():
        import jax, jax.numpy as jnp
        import numpy as np
        N_NODES = 50000
        N_EDGES = 50000
        IN_DIM = 1024
        MID_DIM = 256

        def _gcn_conv(x, W, b, src, dst, norm, n):
            xw = x @ W
            msg = xw[src] * norm[:, None]
            out = jax.ops.segment_sum(msg, dst, num_segments=n)
            return out + b
        key = jax.random.key(seed)
        k1, k2, k3, k4 = jax.random.split(key, 4)
        x = jax.random.normal(k1, (N_NODES, IN_DIM), dtype=jnp.float32)
        edge_index = jax.random.randint(k2, (2, N_EDGES), 0, N_NODES, dtype=jnp.int64)
        W1 = jax.random.normal(k3, (IN_DIM, MID_DIM), dtype=jnp.float32) * (2.0 / (IN_DIM + MID_DIM)) ** 0.5
        W2 = jax.random.normal(k4, (MID_DIM, IN_DIM), dtype=jnp.float32) * (2.0 / (MID_DIM + IN_DIM)) ** 0.5
        b1 = jnp.zeros((MID_DIM,), dtype=jnp.float32)
        b2 = jnp.zeros((IN_DIM,), dtype=jnp.float32)
        return {'x': x, 'edge_index': edge_index, 'W1': W1, 'b1': b1, 'W2': W2, 'b2': b2}
    _L3_gnn_all = _L3_gnn_setup()
    _L3_gnn_in = {k: v for k, v in _L3_gnn_all.items() if k in ('W1', 'b1', 'W2', 'b2')}
    del _L3_gnn_all
    return {'x': x, 'src': src, 'dst': dst, 'edge_type_5': edge_type_5, 'edge_weight': edge_weight, 'L0_gnn_edge_type_weights': _L0_gnn_in['edge_type_weights'], 'L0_gnn_wq': _L0_gnn_in['wq'], 'L0_gnn_bq': _L0_gnn_in['bq'], 'L0_gnn_wk': _L0_gnn_in['wk'], 'L0_gnn_bk': _L0_gnn_in['bk'], 'L0_gnn_wv': _L0_gnn_in['wv'], 'L0_gnn_bv': _L0_gnn_in['bv'], 'L0_gnn_wiq': _L0_gnn_in['wiq'], 'L0_gnn_biq': _L0_gnn_in['biq'], 'L0_gnn_wik': _L0_gnn_in['wik'], 'L0_gnn_bik': _L0_gnn_in['bik'], 'L0_gnn_wiv': _L0_gnn_in['wiv'], 'L0_gnn_biv': _L0_gnn_in['biv'], 'L0_gnn_wo': _L0_gnn_in['wo'], 'L0_gnn_bo': _L0_gnn_in['bo'], 'L1_gnn_bias': _L1_gnn_in['bias'], 'L2_gnn_W': _L2_gnn_in['W'], 'L2_gnn_b': _L2_gnn_in['b'], 'L3_gnn_W1': _L3_gnn_in['W1'], 'L3_gnn_b1': _L3_gnn_in['b1'], 'L3_gnn_W2': _L3_gnn_in['W2'], 'L3_gnn_b2': _L3_gnn_in['b2']}

def reference(x, src, dst, edge_type_5, edge_weight, L0_gnn_edge_type_weights, L0_gnn_wq, L0_gnn_bq, L0_gnn_wk, L0_gnn_bk, L0_gnn_wv, L0_gnn_bv, L0_gnn_wiq, L0_gnn_biq, L0_gnn_wik, L0_gnn_bik, L0_gnn_wiv, L0_gnn_biv, L0_gnn_wo, L0_gnn_bo, L1_gnn_bias, L2_gnn_W, L2_gnn_b, L3_gnn_W1, L3_gnn_b1, L3_gnn_W2, L3_gnn_b2):
    import jax
    import jax.numpy as jnp

    def _L0_gnn_ref(x, edge_index, edge_type, edge_type_weights, wq, bq, wk, bk, wv, bv, wiq, biq, wik, bik, wiv, biv, wo, bo):
        import jax, jax.numpy as jnp
        import numpy as np
        N = 96
        E = 3072
        IN_F = 1024
        OUT_F = 1024
        H = 16
        D = OUT_F // H
        NUM_ETYPES = 4

        def _build_mask(edge_index, edge_type, edge_type_weights, dtype):
            src, dst = (edge_index[0], edge_index[1])
            w = jax.nn.softplus(edge_type_weights)
            mask = jnp.full((N, N), -jnp.inf, dtype=dtype)
            mask = mask.at[src, dst].set(w[edge_type - 1])
            diag = jnp.diagonal(mask)
            idx = jnp.arange(N)
            mask = mask.at[idx, idx].set(jnp.where(jnp.isneginf(diag), w[3], diag))
            return mask
        q = x @ wq.T + bq
        k = x @ wk.T + bk
        v = x @ wv.T + bv
        q2 = (q @ wiq.T + biq).reshape(N, H, D).transpose(1, 0, 2)
        k2 = (k @ wik.T + bik).reshape(N, H, D).transpose(1, 0, 2)
        v2 = (v @ wiv.T + biv).reshape(N, H, D).transpose(1, 0, 2)
        mask = _build_mask(edge_index, edge_type, edge_type_weights, x.dtype)
        scale = 1.0 / np.sqrt(D).astype(np.float32)
        scores = jnp.einsum('hnd,hmd->hnm', q2, k2) * scale + mask[None]
        attn = jax.nn.softmax(scores, axis=-1)
        out = jnp.einsum('hnm,hmd->hnd', attn, v2)
        out = out.transpose(1, 0, 2).reshape(N, OUT_F)
        return out @ wo.T + bo

    def _L1_gnn_ref(x, nnz_weight, bias, edge_index):
        import jax, jax.numpy as jnp
        import numpy as np
        INDIM = 1024
        OUTDIM = 1024
        NNZ = 2048
        N = 50000
        row, col = (edge_index[0], edge_index[1])
        W = jnp.zeros((OUTDIM, INDIM), dtype=nnz_weight.dtype).at[row, col].add(nnz_weight)
        return x @ W.T + bias

    def _L2_gnn_ref(x, edge_index, W, b):
        import jax, jax.numpy as jnp
        import numpy as np
        N = 625
        E = 10000
        D_IN = 1024
        D_OUT = 1024
        num_nodes = x.shape[0]
        self_idx = jnp.arange(num_nodes, dtype=edge_index.dtype)
        ei = jnp.concatenate([edge_index, jnp.stack([self_idx, self_idx], axis=0)], axis=1)
        row, col = (ei[0], ei[1])
        h = jnp.einsum('nd,od->no', x, W) + b
        deg = jnp.zeros((num_nodes,), dtype=h.dtype).at[row].add(1.0)
        deg_inv_sqrt = deg ** (-0.5)
        norm = deg_inv_sqrt[row] * deg_inv_sqrt[col]
        msg = norm[:, None] * h[col]
        out = jax.ops.segment_sum(msg, row, num_segments=num_nodes)
        return out

    def _L3_gnn_ref(x, edge_index, W1, b1, W2, b2):
        import jax, jax.numpy as jnp
        import numpy as np
        N_NODES = 50000
        N_EDGES = 50000
        IN_DIM = 1024
        MID_DIM = 256

        def _gcn_conv(x, W, b, src, dst, norm, n):
            xw = x @ W
            msg = xw[src] * norm[:, None]
            out = jax.ops.segment_sum(msg, dst, num_segments=n)
            return out + b
        n = x.shape[0]
        loops = jnp.arange(n, dtype=edge_index.dtype)
        src = jnp.concatenate([edge_index[0], loops])
        dst = jnp.concatenate([edge_index[1], loops])
        deg = jax.ops.segment_sum(jnp.ones_like(dst, dtype=x.dtype), dst, num_segments=n)
        dis = jnp.where(deg > 0, jax.lax.rsqrt(jnp.maximum(deg, 1.0)), 0.0)
        norm = dis[src] * dis[dst]
        h = jax.nn.relu(_gcn_conv(x, W1, b1, src, dst, norm, n))
        out = _gcn_conv(h, W2, b2, src, dst, norm, n)
        return out
    edge_index = jnp.stack([src, dst])
    h = jnp.maximum(_layernorm(x, axis=-1), 0.0)
    x = x + _L0_gnn_ref(h, edge_index, edge_type_5, L0_gnn_edge_type_weights, L0_gnn_wq, L0_gnn_bq, L0_gnn_wk, L0_gnn_bk, L0_gnn_wv, L0_gnn_bv, L0_gnn_wiq, L0_gnn_biq, L0_gnn_wik, L0_gnn_bik, L0_gnn_wiv, L0_gnn_biv, L0_gnn_wo, L0_gnn_bo)
    h = jnp.maximum(_layernorm(x, axis=-1), 0.0)
    x = x + _L1_gnn_ref(h, edge_weight, L1_gnn_bias, edge_index)
    h = jnp.maximum(_layernorm(x, axis=-1), 0.0)
    x = x + _L2_gnn_ref(h, edge_index, L2_gnn_W, L2_gnn_b)
    h = jnp.maximum(_layernorm(x, axis=-1), 0.0)
    x = x + _L3_gnn_ref(h, edge_index, L3_gnn_W1, L3_gnn_b1, L3_gnn_W2, L3_gnn_b2)
    return x

_drawn_inputs = setup_inputs


def setup_inputs(seed=0):
    import zlib

    import numpy as np

    out = dict(_drawn_inputs(seed))
    spreads = {'L3_gnn_b1': (0.0, 0.1), 'L3_gnn_b2': (0.0, 0.1)}
    factors = {'L0_gnn_edge_type_weights': 64.0,
     'L0_gnn_wq': 8.0,
     'L0_gnn_bq': 8.0,
     'L0_gnn_wk': 8.0,
     'L0_gnn_bk': 64.0,
     'L0_gnn_bv': 7.003,
     'L0_gnn_wiq': 8.0,
     'L0_gnn_biq': 44.852,
     'L0_gnn_wik': 8.0,
     'L0_gnn_bik': 64.0,
     'L0_gnn_biv': 4.515,
     'L0_gnn_bo': 2.792,
     'L2_gnn_b': 6.462}
    for name, (base, spread) in spreads.items():
        noise = np.random.default_rng([zlib.crc32(name.encode()), seed]).standard_normal(out[name].shape)
        drawn = base * np.exp(spread * noise) if base else spread * noise
        out[name] = jnp.asarray(drawn.astype(out[name].dtype))
    for name, factor in factors.items():
        out[name] = (out[name] * factor).astype(out[name].dtype)
    return out
```

```python
from contextlib import ExitStack

import concourse.bass as bass
from concourse import mybir

N = 96
D = 1024
H = 16
DH = D // H
MID = 256
E = 1536
P = 128
KT = D // P
EC = E // P
HALF = 512
ETYPES = 4
EPS = 1e-5
SCALE = DH ** -0.5
NEG = 1.0e30

TPC = 2
CW = TPC * D
LAYERS = ["q", "k", "v", "iq", "ik", "iv", "o", "W"]
CPL = KT // TPC
C_W1 = len(LAYERS) * CPL
C_W2 = C_W1 + 1
NCHUNK = C_W2 + 1
WHOLE = {1, 3, 5, 10, 14, 18, 21}
SPLIT = [c for c in range(NCHUNK) if c not in WHOLE]
RAW_RING = 4
SPLIT_RING = 5


def gnn_kernel(nc, x, weights, bias_t, bias_r, edge_cols, edge_w, edge_rows, type_w, out):
    f32, f32r, bf16, i32 = (mybir.dt.float32, mybir.dt.float32r, mybir.dt.bfloat16, mybir.dt.int32)
    ALU = mybir.AluOpType
    ACT = mybir.ActivationFunctionType
    AX = mybir.AxisListType

    ctx = ExitStack()
    with ctx:
        def sb(name, shape, dt=f32):
            return ctx.enter_context(nc.sbuf_tensor(name, shape, dt))

        def sem(name):
            return ctx.enter_context(nc.semaphore(name))

        raw = sb("raw", [P, RAW_RING, CW])
        w_hi = sb("w_hi", [P, SPLIT_RING, CW], f32r)
        w_lo = sb("w_lo", [P, SPLIT_RING, CW], f32r)
        names = ["h", "q", "k", "v"]
        zf = {n: sb(f"{n}T", [P, KT, N]) for n in names}
        zh = {n: sb(f"{n}T_hi", [P, KT, N], f32r) for n in names}
        zl = {n: sb(f"{n}T_lo", [P, KT, N], f32r) for n in names}
        xa = sb("xa", [N, D])
        xb = sb("xb", [N, D])
        u = sb("u", [N, D])
        y_sb = sb("y_sb", [N, D])
        arena = sb("arena", [P, 5632])
        dst_oh = arena[:, 0:2304].rearrange("p (c a n) -> p c a n", c=EC, a=2)
        src_oh = arena[:, 2304:4608].rearrange("p (c a n) -> p c a n", c=EC, a=2)
        probs = arena[0:N, 0:1536].rearrange("p (h m) -> p h m", h=H)
        probs_t = arena[0:N, 1536:3072].rearrange("p (h m) -> p h m", h=H)
        q2t = arena[:, 3072:3840].rearrange("p (k n) -> p k n", k=KT)
        k2t = arena[:, 3840:4608].rearrange("p (k n) -> p k n", k=KT)
        v2 = arena[0:N, 4608:5632]

        bt = sb("bt", [P, 6, KT])
        br = sb("br", [P, D + MID])
        ecol_i = sb("ecol_i", [P, 3, EC], i32)
        ecol = sb("ecol", [P, 3, EC])
        ew = sb("ew", [P, EC])
        erow_i = sb("erow_i", [2, E], i32)
        erow = y_sb[0:2, :].bitcast(bf16)[:, 0:E]
        coef = sb("coef", [2, P], bf16)
        cell = sb("cell", [P, EC])
        later = zf["k"][:].rearrange("p k n -> p (k n)").bitcast(bf16)
        junk = zf["v"][:].rearrange("p k n -> p (k n)").bitcast(bf16)
        n_later = sb("n_later", [P, EC])
        tw = sb("tw", [P, ETYPES])
        spa = sb("spa", [P, ETYPES])
        spb = sb("spb", [P, ETYPES])
        sp = sb("sp", [P, ETYPES])
        val = sb("val", [P, EC])
        vtmp = sb("vtmp", [P, EC])
        iota_i = sb("iota_i", [P, N], i32)
        iota = sb("iota", [P, N])
        ident = sb("ident", [P, P])
        ones = sb("ones", [P, N])
        eps_t = sb("eps_t", [P, 1])
        unused = sb("unused", [P, 1])
        stats = sb("stats", [N, 4, 3, 6])
        mv = sb("mv", [N, 4, 2])
        std = sb("std", [N, 4])
        rstd = sb("rstd", [N, 4])
        shift0 = sb("shift0", [N, 1])
        cnt = sb("cnt", [N, 2, N])
        deg = sb("deg", [N, 2])
        dsq = sb("dsq", [N, 2])
        dinv = sb("dinv", [N, 2])
        half_a = sb("half_a", [N, 2, N])
        a2t = sb("a2t", [N, N])
        a3t = sb("a3t", [N, N])
        a2s = sb("a2s", [N, N])
        a3s = sb("a3s", [N, N])
        a2_row = sb("a2_row", [1, N])
        w96t = sb("w96t", [N, N])
        mask = sb("mask", [N, N])
        pres = sb("pres", [N, 2, N])
        mx = sb("mx", [N, H])
        sm = sb("sm", [N, H])
        rs = sb("rs", [N, H])
        u1t = sb("u1t", [N, N])
        g = y_sb[:, 0:MID]

        ps = ctx.enter_context(nc.psum_tensor("ps", [P, 8, HALF], f32))

        def place(h):
            return 4 * (2 * (h // 8) + h % 2) + h % 8 // 2

        def y_ps(i):
            return ps[0:N, 2 * i:2 * i + 2, :]

        raw_in = [sem(f"raw_in{i}") for i in range(RAW_RING)]
        hi_done = sem("hi_done")
        lo_done = sem("lo_done")
        chunk_used = sem("chunk_used")
        x_in, bt_in, edge_in, row_in, tw_in, br_in = (sem(n) for n in
            ("x_in", "bt_in", "edge_in", "row_in", "tw_in", "br_in"))
        consts = sem("consts")
        iota_f = sem("iota_f")
        S = {}

        def ev(name):
            if name not in S:
                S[name] = sem(name)
            return S[name]

        y_slot = {"q": 0, "k": 1, "v": 0, "iq": 1, "ik": 0, "iv": 1, "o": 0, "W": 1}
        block = ctx.enter_context(nc.Block())

        def raw_slot(c):
            return c % RAW_RING

        def wait_raw(eng, c):
            eng.wait_ge(raw_in[raw_slot(c)], 16 * (c // RAW_RING + 1))

        def split_index(c):
            return SPLIT.index(c)

        tr_order = ["q", "k", "v", "iq", "ik"]
        bias_of = {"q": 0, "k": 1, "v": 2, "iq": 3, "ik": 4}

        @block.sync
        def _(sp_):
            sp_.dma_start(xa[:], x).then_inc(x_in, 16)
            for c in range(NCHUNK):
                old = c - RAW_RING
                if old >= 0:
                    if old in WHOLE:
                        sp_.wait_ge(chunk_used, old + 1)
                    else:
                        sp_.wait_ge(lo_done, split_index(old) + 1)
                sp_.dma_start(raw[:, raw_slot(c), :], weights[c]).then_inc(raw_in[raw_slot(c)], 16)
            sp_.wait_ge(ev("out_half0"), 1)
            sp_.dma_start(out[:, 0:HALF], xb[:, 0:HALF]).then_inc(ev("stored0"), 16)
            sp_.wait_ge(ev("stored0"), 16)

        def normalize(pool, b):
            pool.wait_ge(ev("row_sum"), b + 1)
            pool.tensor_tensor(probs[:, 4 * b:4 * b + 4, :], probs[:, 4 * b:4 * b + 4, :],
                               rs[:, 4 * b:4 * b + 4].unsqueeze(2).broadcast_to((N, 4, N)),
                               ALU.mult).then_inc(ev("normalized"), 1)

        @block.gpsimd
        def _(pool):
            pool.iota(iota_i[:], pattern=[[1, N]], base=0, channel_multiplier=0).then_inc(consts, 1)
            pool.memset(ident[:], 0.0).then_inc(consts, 1)
            pool.memset(later, 1.0).then_inc(consts, 1)
            pool.wait_ge(consts, 3)
            pool.affine_select(out=ident[:], in_=ident[:], compare_op=ALU.not_equal, fill=1.0, base=0,
                               pattern=[[-1, P]], channel_multiplier=1).then_inc(consts, 1)
            pool.affine_select(out=later[:, 0:P], in_=later[:, 0:P], compare_op=ALU.is_gt, fill=0.0, base=0,
                               pattern=[[1, P]], channel_multiplier=-1).then_inc(consts, 1)
            pool.wait_ge(ev("onehots"), 2)
            pool.tensor_tensor(src_oh[:, :, 1, :], src_oh[:, :, 0, :],
                               ew[:].unsqueeze(2).broadcast_to((P, EC, N)), ALU.mult).then_inc(ev("w_rows"), 1)
            pool.wait_ge(ev("val_ready"), 1)
            pool.tensor_tensor(dst_oh[:, :, 1, :], dst_oh[:, :, 0, :],
                               val[:].unsqueeze(2).broadcast_to((P, EC, N)), ALU.mult).then_inc(ev("v_rows"), 1)
            for b in range(4):
                pool.wait_ge(ev("row_max"), b + 1)
                pool.tensor_tensor(probs[:, 4 * b:4 * b + 4, :], probs[:, 4 * b:4 * b + 4, :],
                                   mx[:, 4 * b:4 * b + 4].unsqueeze(2).broadcast_to((N, 4, N)),
                                   ALU.subtract).then_inc(ev("shifted"), 1)
                if b >= 1:
                    normalize(pool, b - 1)
            normalize(pool, 3)

        @block.scalar
        def _(act):
            act.dma_start(tw[:], type_w).then_inc(tw_in, 16)
            act.dma_start(erow_i[:], edge_rows).then_inc(row_in, 16)
            act.dma_start(ecol_i[:], edge_cols).then_inc(edge_in, 16)
            act.dma_start(ew[:], edge_w).then_inc(edge_in, 16)
            act.dma_start(bt[:], bias_t).then_inc(bt_in, 16)
            act.dma_start(br[0:P:32, :], bias_r).then_inc(br_in, 16)

            def split(c):
                if c in WHOLE:
                    return
                i = split_index(c)
                wait_raw(act, c)
                if i >= SPLIT_RING:
                    act.wait_ge(chunk_used, SPLIT[i - SPLIT_RING] + 1)
                act.activation(w_hi[:, i % SPLIT_RING, :], raw[:, raw_slot(c), :], ACT.Copy).then_inc(hi_done, 1)

            def evacuate(name):
                li = LAYERS.index(name)
                act.wait_ge(chunk_used, CPL * (li + 1))
                if name == "iv":
                    for hf in range(2):
                        act.activation(v2[:, hf * HALF:(hf + 1) * HALF], y_ps(y_slot[name])[:, hf, :],
                                       ACT.Copy).then_inc(ev("y_iv"), 1)
                    return
                i = tr_order.index(name)
                if i:
                    act.wait_ge(ev(f"tr_{tr_order[i - 1]}"), 2)
                for hf in range(2):
                    act.activation(y_sb[:, hf * HALF:(hf + 1) * HALF], y_ps(y_slot[name])[:, hf, :],
                                   ACT.Copy).then_inc(ev(f"y_{name}"), 1)

            def leading(name, src=None):
                for b in range(2):
                    act.wait_ge(ev(f"{name}T_f"), b + 1)
                    act.activation(zh[name][:, 4 * b:4 * b + 4, :], zf[name][:, 4 * b:4 * b + 4, :],
                                   ACT.Copy).then_inc(ev(f"{name}T_h"), 1)

            def root(i):
                act.wait_ge(ev(f"mv{i}"), 1)
                act.activation(std[:, i:i + 1], mv[:, i, 1:2], ACT.Sqrt, bias=eps_t[0:N, :]).then_inc(ev(f"std{i}"), 1)

            act.wait_ge(ev("neg_abs"), 1)
            act.activation(spb[:], spa[:], ACT.Exp).then_inc(ev("sp_exp"), 1)
            act.wait_ge(ev("sp_exp"), 1)
            act.activation(sp[:], spb[:], ACT.Ln, bias=1.0).then_inc(ev("sp_ln"), 1)
            act.wait_ge(ev("eps"), 1)
            root(0)
            act.wait_ge(ev("shift0"), 1)
            for hf in range(2):
                s = slice(hf * HALF, (hf + 1) * HALF)
                act.activation(u[:, s], xa[:, s], ACT.Relu, bias=shift0[:], scale=rstd[:, 0:1]).then_inc(ev("h0"), 1)
            split(0)
            leading("h")
            for c in range(1, 6):
                split(c)
            evacuate("q")
            split(6)
            split(7)
            leading("q")
            act.wait_ge(ev("deg"), 1)
            act.activation(dsq[:], deg[:], ACT.Sqrt).then_inc(ev("dsq"), 1)
            split(8)
            split(9)
            evacuate("k")
            split(10)
            split(11)
            leading("k")
            split(12)
            split(13)
            evacuate("v")
            split(14)
            split(15)
            leading("v")
            split(16)
            split(17)
            evacuate("iq")
            for c in range(18, 22):
                split(c)
            evacuate("ik")
            split(22)
            split(23)
            for b in range(4):
                act.wait_ge(ev("shifted"), b + 1)
                act.activation(probs[:, 4 * b:4 * b + 4, :], probs[:, 4 * b:4 * b + 4, :], ACT.Exp).then_inc(ev("exps"), 1)
            split(24)
            act.activation(unused[:], eps_t[:], ACT.Sqrt)
            evacuate("iv")
            for b in range(4):
                act.wait_ge(ev("probs_tr"), b + 1)
                act.activation(probs_t[:, 4 * b:4 * b + 4, :], ps[0:N, 4 + b, 0:4 * N].rearrange("p (h m) -> p h m", h=4),
                               ACT.Copy).then_inc(ev("probs_t"), 1)
            split(25)

            for b in range(4):
                act.wait_ge(ev("attn_f"), b + 1)
                if b == 0:
                    act.wait_ge(chunk_used, 3 * CPL)
                act.activation(zh["h"][:, 2 * b:2 * b + 2, :], zf["h"][:, 2 * b:2 * b + 2, :],
                               ACT.Copy).then_inc(ev("attn_h"), 1)
            split(26)
            split(27)
            split(28)
            root(1)
            split(29)
            root(2)

            def leading_ps(name, key, tiles, per_bank):
                for b in range(tiles // per_bank):
                    act.wait_ge(ev(f"{key}_mm"), b + 1)
                    src = ps[:, 4 + b, 0:per_bank * N].rearrange("p (k n) -> p k n", k=per_bank)
                    act.activation(zh[name][:, per_bank * b:per_bank * (b + 1), :], src,
                                   ACT.Copy).then_inc(ev(f"{key}_h"), 1)

            leading_ps("q", "ah2", KT, 2)
            for c in range(30, 33):
                split(c)
            root(3)
            leading_ps("k", "ah3", KT, 2)
            split(33)
            act.wait_ge(ev("g_mm"), 1)
            act.activation(g, ps[0:N, 0, 0:MID], ACT.Relu).then_inc(ev("g"), 1)
            leading_ps("v", "ag", 2, 1)
            act.wait_ge(ev("out_half1"), 1)
            act.dma_start(out[:, HALF:D], xb[:, HALF:D]).then_inc(ev("stored1"), 16)
            act.wait_ge(ev("stored1"), 16)

        @block.vector
        def _(dve):
            done = sem("dve_chain")
            chain = [0]

            def link(ins):
                chain[0] += 1
                ins.then_inc(done, 1)
                dve.wait_ge(done, chain[0])

            def split(c):
                if c in WHOLE:
                    return
                i = split_index(c)
                dve.wait_ge(hi_done, i + 1)
                dve.tensor_tensor(w_lo[:, i % SPLIT_RING, :], raw[:, raw_slot(c), :],
                                  w_hi[:, i % SPLIT_RING, :].bitcast(f32), ALU.subtract).then_inc(lo_done, 1)

            def add_bias(name, dst, banks):
                for b in range(2):
                    dve.wait_ge(ev(f"tr_{name}"), b + 1)
                    dve.tensor_tensor(dst[:, 4 * b:4 * b + 4, :],
                                      ps[:, banks[b], 0:4 * N].rearrange("p (k n) -> p k n", k=4),
                                      bt[:, bias_of[name], 4 * b:4 * b + 4].unsqueeze(2).broadcast_to((P, 4, N)),
                                      ALU.add).then_inc(ev(f"{name}T_f"), 1)

            def rest(name):
                for b in range(2):
                    dve.wait_ge(ev(f"{name}T_h"), b + 1)
                    s = slice(4 * b, 4 * b + 4)
                    dve.tensor_tensor(zl[name][:, s, :], zf[name][:, s, :], zh[name][:, s, :].bitcast(f32),
                                      ALU.subtract).then_inc(ev(f"{name}T_l"), 1)

            def bn(i, seg, xt, a, b):
                return dve.bn_stats(stats[:, i, seg, :], xt[:, a:b])

            def aggregate(i, nseg):
                dve.bn_aggr(mv[:, i, :], stats[:, i, 0:nseg, :]).then_inc(ev(f"mv{i}"), 1)

            def reciprocal_std(i):
                dve.wait_ge(ev(f"std{i}"), 1)
                link(dve.reciprocal(rstd[:, i:i + 1], std[:, i:i + 1]))

            dve.memset(eps_t[:], EPS).then_inc(ev("eps"), 1)
            dve.memset(ones[:], 1.0).then_inc(ev("ones"), 1)
            link(dve.memset(coef[:], 1.0))
            dve.memset(coef[0:1, :], float(N)).then_inc(ev("coef"), 1)
            dve.wait_ge(tw_in, 16)
            link(dve.tensor_scalar(spa[:], tw[:], -1.0, None, ALU.mult))
            dve.tensor_tensor(spa[:], spa[:], tw[:], ALU.min).then_inc(ev("neg_abs"), 1)
            dve.wait_ge(row_in, 16)
            dve.tensor_copy(erow, erow_i[:]).then_inc(ev("erow"), 1)
            dve.wait_ge(x_in, 16)
            link(bn(0, 0, xa, 0, HALF))
            link(bn(0, 1, xa, HALF, D))
            aggregate(0, 2)
            dve.wait_ge(edge_in, 32)
            link(dve.tensor_copy(ecol[:], ecol_i[:]))
            link(dve.tensor_scalar(vtmp[:], ecol[:, 0, :], float(N), None, ALU.mult))
            link(dve.tensor_tensor(cell[:], vtmp[:], ecol[:, 1, :], ALU.add))
            dve.wait_ge(consts, 5)
            link(dve.tensor_copy(iota[:], iota_i[:]))
            reciprocal_std(0)
            dve.wait_ge(ev("mv0"), 1)
            dve.tensor_scalar(shift0[:], mv[:, 0, 0:1], rstd[:, 0:1], -1.0, ALU.mult, ALU.mult).then_inc(ev("shift0"), 1)
            for k, oh in ((0, src_oh), (1, dst_oh)):
                dve.tensor_tensor(oh[:, :, 0, :], iota[:].unsqueeze(1).broadcast_to((P, EC, N)),
                                  ecol[:, k, :].unsqueeze(2).broadcast_to((P, EC, N)),
                                  ALU.is_equal).then_inc(ev("onehots"), 1)
            for b in range(2):
                dve.wait_ge(ev("tr_h"), b + 1)
                dve.tensor_copy(zf["h"][:, 4 * b:4 * b + 4, :],
                                ps[:, 2 + b, 0:4 * N].rearrange("p (k n) -> p k n", k=4)).then_inc(ev("hT_f"), 1)
            rest("h")
            split(0)

            def count_later(c):
                dve.scalar_tensor_tensor(out=junk[:, 0:E - P * c], in0=cells_ps[:, P * c:E], scalar=cell[:, c:c + 1],
                                         in1=later[:, 0:E - P * c], op0=ALU.is_equal, op1=ALU.mult,
                                         accum_out=n_later[:, c:c + 1]).then_inc(ev("counted"), 1)

            cells_ps = ps[:, 5:8, :].rearrange("p b n -> p (b n)")
            dve.wait_ge(ev("cells"), 1)
            split(1)
            for c in range(EC):
                if c:
                    dve.wait_ge(ev("counted"), c)
                count_later(c)
                if c == 2:
                    split(2)
                if c == 5:
                    split(3)
                if c == 8:
                    split(4)
            dve.wait_ge(ev("sp_ln"), 1)
            link(dve.tensor_scalar(spa[:], tw[:], 0.0, None, ALU.max))
            link(dve.tensor_tensor(sp[:], sp[:], spa[:], ALU.add))
            for t in range(ETYPES + 1):
                k = (t - 1) % ETYPES
                if t == 0:
                    link(dve.tensor_scalar(val[:], ecol[:, 2, :], float(t), sp[:, k:k + 1], ALU.is_equal, ALU.mult))
                else:
                    link(dve.tensor_scalar(vtmp[:], ecol[:, 2, :], float(t), sp[:, k:k + 1], ALU.is_equal, ALU.mult))
                    link(dve.tensor_tensor(val[:], val[:], vtmp[:], ALU.add))
            dve.wait_ge(ev("counted"), EC)
            link(dve.tensor_scalar(vtmp[:], n_later[:], 0.0, None, ALU.is_equal))
            dve.tensor_tensor(val[:], val[:], vtmp[:], ALU.mult).then_inc(ev("val_ready"), 1)
            split(5)
            split(6)
            dve.wait_ge(bt_in, 16)
            add_bias("q", zf["q"], (4, 7))
            rest("q")

            dve.wait_ge(ev("graph_mm"), 2)
            for i in range(2):
                link(dve.tensor_tensor(cnt[:, i, :], ps[0:N, 5 + i, 0:N], ident[0:N, 0:N], ALU.add))
            dve.tensor_reduce(deg[:], cnt[:], AX.X, ALU.add).then_inc(ev("deg"), 1)
            link(dve.tensor_copy(w96t[:], ps[0:N, 6, N:2 * N]))
            link(dve.tensor_tensor(mask[:], cnt[:, 0, :], ident[0:N, 0:N], ALU.subtract))
            link(dve.tensor_scalar(mask[:], mask[:], 1.0, None, ALU.min))
            link(dve.scalar_tensor_tensor(out=pres[:, 0, :], in0=mask[:], scalar=-1.0, in1=ident[0:N, 0:N],
                                          op0=ALU.add, op1=ALU.mult))
            link(dve.tensor_scalar(pres[:, 0, :], pres[:, 0, :], sp[0:N, 3:4], -1.0, ALU.mult, ALU.mult))
            link(dve.tensor_scalar(pres[:, 1, :], cnt[:, 0, :], 1.0, 1.0, ALU.min, ALU.subtract))
            link(dve.scalar_tensor_tensor(out=pres[:, 0, :], in0=pres[:, 1, :], scalar=NEG, in1=pres[:, 0, :],
                                          op0=ALU.mult, op1=ALU.add))
            link(dve.tensor_tensor(mask[:], pres[:, 0, :], ps[0:N, 5, N:2 * N], ALU.add))
            split(7)
            dve.wait_ge(ev("dsq"), 1)
            link(dve.reciprocal(dinv[:], dsq[:]))
            for i in range(2):
                dve.tensor_scalar(half_a[:, i, :], cnt[:, i, :], dinv[:, i:i + 1], None,
                                  ALU.mult).then_inc(ev("half_a"), 1)
            split(8)
            dve.wait_ge(ev("half_tr"), 2)
            dve.tensor_scalar(a2t[:], ps[0:N, 5, 2 * N:3 * N], dinv[:, 0:1], None, ALU.mult).then_inc(ev("adjacency"), 1)
            dve.tensor_scalar(a3t[:], ps[0:N, 5, 3 * N:4 * N], dinv[:, 1:2], None, ALU.mult).then_inc(ev("adjacency"), 1)
            split(9)
            add_bias("k", zf["k"], (4, 7))
            split(10)
            rest("k")
            dve.wait_ge(ev("row_mm"), 1)
            dve.tensor_copy(a2_row[:], ps[0:1, 6, 2 * N:3 * N]).then_inc(ev("a2_row"), 1)
            for c in range(11, 14):
                split(c)
            add_bias("v", zf["v"], (4, 7))
            split(14)
            rest("v")
            for c in range(15, 18):
                split(c)
            dve.wait_ge(ev("w_rows"), 1)
            add_bias("iq", q2t, (4, 5))
            for c in range(18, 22):
                split(c)
            add_bias("ik", k2t, (6, 7))
            split(22)
            split(23)

            def row_sums(b):
                s = slice(4 * b, 4 * b + 4)
                dve.wait_ge(ev("exps"), b + 1)
                link(dve.reduce_sum(sm[:, s], probs[:, s, :], AX.X))
                dve.reciprocal(rs[:, s], sm[:, s]).then_inc(ev("row_sum"), 1)

            for b in range(4):
                s = slice(4 * b, 4 * b + 4)
                dve.wait_ge(ev("scores"), b + 1)
                link(dve.scalar_tensor_tensor(out=probs[:, s, :],
                                              in0=ps[0:N, 4 + b, 0:4 * N].rearrange("p (h m) -> p h m", h=4),
                                              scalar=SCALE, in1=mask[:].unsqueeze(1).broadcast_to((N, 4, N)),
                                              op0=ALU.mult, op1=ALU.add))
                dve.reduce_max(mx[:, s], probs[:, s, :], AX.X).then_inc(ev("row_max"), 1)
            for b in range(4):
                row_sums(b)
            split(24)

            def attn_rest(b):
                s = slice(2 * b, 2 * b + 2)
                dve.wait_ge(ev("attn_h"), b + 1)
                dve.tensor_tensor(zl["h"][:, s, :], zf["h"][:, s, :], zh["h"][:, s, :].bitcast(f32),
                                  ALU.subtract).then_inc(ev("attn_l"), 1)

            split(25)
            for b in range(4):
                s = slice(2 * b, 2 * b + 2)
                dve.wait_ge(ev("attn_mm"), b + 1)
                dve.tensor_tensor(zf["h"][:, s, :], ps[:, 4 + b, 0:2 * N].rearrange("p (k n) -> p k n", k=2),
                                  bt[:, 5, s].unsqueeze(2).broadcast_to((P, 2, N)), ALU.add).then_inc(ev("attn_f"), 1)
                if b:
                    attn_rest(b - 1)
            attn_rest(3)
            split(26)
            split(27)

            H0, H1 = slice(0, HALF), slice(HALF, D)
            dve.wait_ge(ev("o_half"), 1)
            link(dve.tensor_tensor(xa[:, H0], y_ps(0)[:, 0, :], xa[:, H0], ALU.add))
            link(bn(1, 0, xa, 0, HALF))
            dve.wait_ge(ev("l1_bias"), 1)
            link(dve.tensor_tensor(xb[:, H0], y_ps(1)[:, 0, :], xa[:, H0], ALU.add))
            link(bn(2, 0, xb, N, HALF))
            split(28)
            dve.wait_ge(ev("o_half"), 2)
            link(dve.tensor_tensor(xa[:, H1], y_ps(0)[:, 1, :], xa[:, H1], ALU.add))
            link(bn(1, 1, xa, HALF, D))
            aggregate(1, 2)
            dve.wait_ge(ev("mv1"), 1)
            dve.tensor_scalar(u[:, 0:N], xa[:, 0:N], mv[:, 1, 0:1], 0.0, ALU.subtract, ALU.max).then_inc(ev("u1"), 1)
            reciprocal_std(1)
            dve.wait_ge(ev("tr_u1"), 1)
            dve.tensor_copy(u1t[:], ps[0:N, 4, 0:N]).then_inc(ev("u1t"), 1)
            link(dve.tensor_tensor(xb[:, H1], y_ps(1)[:, 1, :], xa[:, H1], ALU.add))
            link(bn(2, 1, xb, HALF, D))
            dve.wait_ge(ev("l1_mm"), 1)
            link(dve.scalar_tensor_tensor(out=xb[:, 0:N], in0=ps[0:N, 5, 0:N], scalar=rstd[:, 1:2], in1=xb[:, 0:N],
                                          op0=ALU.mult, op1=ALU.add))
            link(bn(2, 2, xb, 0, N))

            def norm_and_scale(i, nseg, xt, at, a_scaled, key):
                aggregate(i, nseg)
                dve.wait_ge(ev(f"mv{i}"), 1)
                dve.tensor_scalar(u[:, H0], xt[:, H0], mv[:, i, 0:1], 0.0, ALU.subtract, ALU.max)\
                   .then_inc(ev(f"u_{key}"), 1)
                reciprocal_std(i)
                dve.tensor_scalar(a_scaled[:], at[:], rstd[:, i:i + 1], None, ALU.mult).then_inc(ev(f"as_{key}"), 1)
                dve.tensor_scalar(u[:, H1], xt[:, H1], mv[:, i, 0:1], 0.0, ALU.subtract, ALU.max)\
                   .then_inc(ev(f"u_{key}"), 1)

            def rest_ps(name, key, tiles, per_bank):
                for b in range(tiles // per_bank):
                    s = slice(per_bank * b, per_bank * (b + 1))
                    dve.wait_ge(ev(f"{key}_h"), b + 1)
                    dve.tensor_tensor(zl[name][:, s, :], ps[:, 4 + b, 0:per_bank * N].rearrange("p (k n) -> p k n", k=per_bank),
                                      zh[name][:, s, :].bitcast(f32), ALU.subtract).then_inc(ev(f"{key}_l"), 1)

            norm_and_scale(2, 3, xb, a2t, a2s, "2")
            split(29)
            rest_ps("q", "ah2", KT, 2)
            split(30)
            split(31)
            for hf, s in enumerate((H0, H1)):
                dve.wait_ge(ev("W_half"), hf + 1)
                link(dve.tensor_tensor(xa[:, s], y_ps(1)[:, hf, :], xb[:, s], ALU.add))
                link(bn(3, hf, xa, hf * HALF, (hf + 1) * HALF))
                if hf == 0:
                    split(32)
            norm_and_scale(3, 2, xa, a3t, a3s, "3")
            rest_ps("k", "ah3", KT, 2)
            split(33)
            rest_ps("v", "ag", 2, 1)
            for hf, s in enumerate((H0, H1)):
                dve.wait_ge(ev("W2_half"), hf + 1)
                dve.tensor_tensor(xb[:, s], y_ps(1)[:, hf, :], xa[:, s], ALU.add).then_inc(ev(f"out_half{hf}"), 1)

        @block.tensor
        def _(pe):
            def mm(o, l, r, start, stop):
                return pe.matmul(o, l, r, start=start, stop=stop)

            def chunk(name, c, z, key=None):
                j = c % CPL
                acc = y_ps(y_slot[name])
                if c in WHOLE:
                    wait_raw(pe, c)
                    w = raw[:, raw_slot(c), :].rearrange("p (t n) -> p t n", t=TPC)
                    parts = [(zf[z], w)]
                else:
                    i = split_index(c)
                    pe.wait_ge(lo_done, i + 1)
                    hi = w_hi[:, i % SPLIT_RING, :].rearrange("p (t n) -> p t n", t=TPC)
                    lo = w_lo[:, i % SPLIT_RING, :].rearrange("p (t n) -> p t n", t=TPC)
                    parts = [(zh[z], hi), (zh[z], lo), (zl[z], hi)]
                for t in range(TPC):
                    kt = TPC * j + t
                    for pi, (zp, w) in enumerate(parts):
                        for hf in range(2):
                            last = mm(acc[:, hf, :], zp[:, kt, :], w[:, t, hf * HALF:(hf + 1) * HALF],
                                      kt == 0 and pi == 0, kt == KT - 1 and pi == len(parts) - 1)
                last.then_inc(chunk_used, 1)

            def transposes(name, banks):
                for b in range(2):
                    pe.wait_ge(ev(f"y_{name}"), b + 1)
                    for k in range(4):
                        kt = 4 * b + k
                        last = pe.transpose(ps[:, banks[b], k * N:(k + 1) * N], y_sb[:, kt * P:(kt + 1) * P],
                                            ident[0:N, 0:N])
                    last.then_inc(ev(f"tr_{name}"), 1)

            pe.wait_ge(ev("coef"), 1)
            pe.wait_ge(ev("erow"), 1)
            for b in range(3):
                last = mm(ps[:, 5 + b, :], coef[:], erow[:, b * HALF:(b + 1) * HALF], True, True)
            last.then_inc(ev("cells"), 1)
            pe.wait_ge(consts, 5)
            for b in range(2):
                pe.wait_ge(ev("h0"), b + 1)
                for k in range(4):
                    kt = 4 * b + k
                    last = pe.transpose(ps[:, 2 + b, k * N:(k + 1) * N], u[:, kt * P:(kt + 1) * P], ident[0:N, 0:N])
                last.then_inc(ev("tr_h"), 1)

            pe.wait_ge(ev("hT_l"), 2)
            for c in range(0, 4):
                chunk("q", c, "h")
            pe.wait_ge(ev("w_rows"), 1)
            pe.wait_ge(ev("v_rows"), 1)
            for i, (l, r) in enumerate(((src_oh, dst_oh), (dst_oh, src_oh))):
                for c in range(EC):
                    last = mm(ps[0:N, 5 + i, 0:2 * N], l[:, c, 0, :], r[:, c, :, :].rearrange("p a n -> p (a n)"),
                              c == 0, c == EC - 1)
                last.then_inc(ev("graph_mm"), 1)
            chunk("k", 4, "h")
            transposes("q", (4, 7))
            for c in range(5, 8):
                chunk("k", c, "h")
            pe.wait_ge(ev("half_a"), 2)
            for i in range(2):
                last = pe.transpose(ps[0:N, 5, (2 + i) * N:(3 + i) * N], half_a[:, i, :], ident[0:N, 0:N])
                last.then_inc(ev("half_tr"), 1)
            chunk("v", 8, "h")
            pe.wait_ge(ev("qT_f"), 2)
            transposes("k", (4, 7))
            pe.wait_ge(ev("adjacency"), 2)
            pe.wait_ge(ev("ones"), 1)
            mm(ps[0:1, 6, 2 * N:3 * N], ones[0:N, 0:1], a2t[:], True, True).then_inc(ev("row_mm"), 1)
            for c in range(9, 12):
                chunk("v", c, "h")
            pe.wait_ge(ev("qT_l"), 2)
            pe.wait_ge(ev("y_k"), 2)
            chunk("iq", 12, "q")
            pe.wait_ge(ev("kT_f"), 2)
            transposes("v", (4, 7))
            for c in range(13, 16):
                chunk("iq", c, "q")
            pe.wait_ge(ev("kT_l"), 2)
            pe.wait_ge(ev("y_v"), 2)
            chunk("ik", 16, "k")
            pe.wait_ge(ev("vT_f"), 2)
            transposes("iq", (4, 5))
            for c in range(17, 20):
                chunk("ik", c, "k")
            pe.wait_ge(ev("vT_l"), 2)
            pe.wait_ge(ev("y_iq"), 2)
            pe.wait_ge(ev("a2_row"), 1)
            chunk("iv", 20, "v")
            transposes("ik", (6, 7))
            chunk("iv", 21, "v")
            pe.wait_ge(ev("iqT_f"), 2)
            pe.wait_ge(ev("ikT_f"), 2)
            for pair in range(2):
                for k in range(4):
                    for odd in range(2):
                        kt = 4 * pair + k
                        r = slice(DH * odd, DH * odd + DH)
                        last = mm(ps[0:N, 4 + 2 * pair + odd, k * N:(k + 1) * N], q2t[r, kt, :], k2t[r, kt, :], True, True)
                        if k == 3:
                            last.then_inc(ev("scores"), 1)
            chunk("iv", 22, "v")
            chunk("iv", 23, "v")
            for b in range(4):
                pe.wait_ge(ev("normalized"), b + 1)
                for k in range(4):
                    last = pe.transpose(ps[0:N, 4 + b, k * N:(k + 1) * N], probs[:, 4 * b + k, :], ident[0:N, 0:N])
                last.then_inc(ev("probs_tr"), 1)
            pe.wait_ge(br_in, 16)
            pe.wait_ge(ev("y_ik"), 2)
            for hf in range(2):
                s = slice(hf * HALF, (hf + 1) * HALF)
                mm(y_ps(0)[:, hf, :], ones[32:33, :], br[32:33, s], True, False)
            pe.wait_ge(ev("y_iv"), 2)
            for b in range(4):
                pe.wait_ge(ev("probs_t"), 2 * (b // 2) + 2)
                for k in range(4):
                    h = 4 * b + k
                    r = slice(DH * (h % 2), DH * (h % 2) + DH)
                    c0 = (k // 2) * N
                    last = mm(ps[r, 4 + b, c0:c0 + N], v2[:, h * DH:(h + 1) * DH], probs_t[:, place(h), :], True, True)
                last.then_inc(ev("attn_mm"), 1)
            for hf in range(2):
                s = slice(hf * HALF, (hf + 1) * HALF)
                last = mm(y_ps(1)[:, hf, :], ones[64:65, :], br[64:65, s], True, True)
            last.then_inc(ev("l1_bias"), 1)

            def layer_by_halves(slot, c0, tiles, z, parts_sem, per, half_sem):
                for hf in range(2):
                    for kt in range(tiles):
                        c = c0 + kt // TPC
                        i = split_index(c)
                        if hf == 0 and kt % TPC == 0:
                            pe.wait_ge(lo_done, i + 1)
                        if hf == 0 and kt % per == 0:
                            pe.wait_ge(parts_sem, kt // per + 1)
                        s = slice((kt % TPC) * D + hf * HALF, (kt % TPC) * D + (hf + 1) * HALF)
                        hi, lo = w_hi[:, i % SPLIT_RING, s], w_lo[:, i % SPLIT_RING, s]
                        acc = y_ps(slot)[:, hf, :]
                        mm(acc, zh[z][:, kt, :], hi, False, False)
                        mm(acc, zh[z][:, kt, :], lo, False, False)
                        last = mm(acc, zl[z][:, kt, :], hi, False, kt == tiles - 1)
                        if kt == tiles - 1:
                            last.then_inc(half_sem, 1)
                        elif hf == 1 and kt % TPC == TPC - 1:
                            last.then_inc(chunk_used, 1)
                pe.wait_ge(half_sem, 2)
                pe.nop().then_inc(chunk_used, 1)

            layer_by_halves(0, 6 * CPL, KT, "h", ev("attn_l"), 2, ev("o_half"))
            pe.wait_ge(ev("u1"), 1)
            pe.transpose(ps[0:N, 4, 0:N], u[:, 0:N], ident[0:N, 0:N]).then_inc(ev("tr_u1"), 1)
            pe.wait_ge(ev("u1t"), 1)
            mm(ps[0:N, 5, 0:N], u1t[:], w96t[:], True, True).then_inc(ev("l1_mm"), 1)

            def aggregation(key, a_scaled):
                pe.wait_ge(ev(f"as_{key}"), 1)
                for b in range(4):
                    pe.wait_ge(ev(f"u_{key}"), b // 2 + 1)
                    for k in range(2):
                        kt = 2 * b + k
                        last = mm(ps[:, 4 + b, k * N:(k + 1) * N], u[:, kt * P:(kt + 1) * P], a_scaled[:], True, True)
                    last.then_inc(ev(f"ah{key}_mm"), 1)

            pe.wait_ge(ev("u_2"), 1)
            for hf in range(2):
                mm(y_ps(1)[:, hf, :], a2_row[:], br[0:1, hf * HALF:(hf + 1) * HALF], True, False)
            aggregation("2", a2s)
            layer_by_halves(1, 7 * CPL, KT, "q", ev("ah2_l"), 2, ev("W_half"))
            mm(ps[0:N, 0, 0:MID], ones[0:1, :], br[0:1, D:D + MID], True, False)
            aggregation("3", a3s)
            i = split_index(C_W1)
            pe.wait_ge(lo_done, i + 1)
            for kt in range(KT):
                if kt % 2 == 0:
                    pe.wait_ge(ev("ah3_l"), kt // 2 + 1)
                s = slice(kt * MID, (kt + 1) * MID)
                hi, lo = w_hi[:, i % SPLIT_RING, s], w_lo[:, i % SPLIT_RING, s]
                mm(ps[0:N, 0, 0:MID], zh["k"][:, kt, :], hi, False, False)
                mm(ps[0:N, 0, 0:MID], zh["k"][:, kt, :], lo, False, False)
                last = mm(ps[0:N, 0, 0:MID], zl["k"][:, kt, :], hi, False, kt == KT - 1)
            last.then_inc(ev("g_mm"), 1)
            for hf in range(2):
                mm(y_ps(1)[:, hf, :], ones[96:97, :], br[96:97, hf * HALF:(hf + 1) * HALF], True, False)
            pe.wait_ge(ev("g"), 1)
            for k in range(2):
                mm(ps[:, 4 + k, 0:N], g[:, k * P:(k + 1) * P], a3t[:], True, True).then_inc(ev("ag_mm"), 1)
            layer_by_halves(1, C_W2, MID // P, "v", ev("ag_l"), 1, ev("W2_half"))


def kernel(**inputs):
    import numpy as np
    import concourse.bacc as bacc
    from concourse.bass_utils import run_bass_kernel_spmd

    a = {k: np.asarray(v) for k, v in inputs.items()}

    def chunks(w_kn):
        k, n = w_kn.shape
        return w_kn.reshape(k // (TPC * P), TPC, P, n).transpose(0, 2, 1, 3).reshape(-1, P, TPC * n)

    full = ["L0_gnn_wq", "L0_gnn_wk", "L0_gnn_wv", "L0_gnn_wiq", "L0_gnn_wik", "L0_gnn_wiv", "L0_gnn_wo", "L2_gnn_W"]
    w1 = a["L3_gnn_W1"].reshape(KT, P, MID).transpose(1, 0, 2).reshape(1, P, CW)
    weights = np.ascontiguousarray(np.concatenate([chunks(a[n].T) for n in full] + [w1, chunks(a["L3_gnn_W2"])]))
    cols = ["L0_gnn_bq", "L0_gnn_bk", "L0_gnn_bv", "L0_gnn_biq", "L0_gnn_bik", "L0_gnn_biv"]
    bias_t = np.ascontiguousarray(np.stack([a[n].reshape(KT, P).T for n in cols], axis=1))
    bias_r = np.zeros((4, D + MID), a["L2_gnn_b"].dtype)
    for i, n in enumerate(["L2_gnn_b", "L0_gnn_bo", "L1_gnn_bias", "L3_gnn_b2"]):
        bias_r[i, 0:D] = a[n]
    bias_r[0, D:] = a["L3_gnn_b1"]
    edge_cols = np.ascontiguousarray(np.stack([a[n].reshape(EC, P).T for n in ("src", "dst", "edge_type_5")], axis=1))
    arrays = {
        "x": a["x"], "weights": weights, "bias_t": bias_t, "bias_r": bias_r, "edge_cols": edge_cols,
        "edge_w": np.ascontiguousarray(a["edge_weight"].reshape(EC, P).T),
        "edge_rows": np.ascontiguousarray(np.stack([a["src"], a["dst"]])),
        "type_w": np.ascontiguousarray(np.broadcast_to(a["L0_gnn_edge_type_weights"], (P, ETYPES))),
    }
    nc = bacc.Bacc("TRN2", target_bir_lowering=False, num_devices=1)
    aps = [nc.dram_tensor(n, v.shape, mybir.dt.from_np(v.dtype), kind="ExternalInput").ap() for n, v in arrays.items()]
    out = nc.dram_tensor("out", (N, D), mybir.dt.float32, kind="ExternalOutput").ap()
    gnn_kernel(nc, *aps, out)
    r = run_bass_kernel_spmd(nc, [arrays], core_ids=[0])
    return r.results[0]["out"]
```

```python
from contextlib import ExitStack

import concourse.bass as bass
from concourse import mybir

N = 96
D = 1024
H = 16
DH = D // H
MID = 256
E = 1536
P = 128
KT = D // P
EC = E // P
HALF = 512
ETYPES = 4
EPS = 1e-5
SCALE = DH ** -0.5
NEG = 1.0e30

TPC = 2
CW = TPC * D
LAYERS = ["q", "k", "v", "iq", "ik", "iv", "o", "W"]
CPL = KT // TPC
C_W1 = len(LAYERS) * CPL
C_W2 = C_W1 + 1
NCHUNK = C_W2 + 1
WHOLE = {0, 1, 4}
SPLIT = [c for c in range(NCHUNK) if c not in WHOLE]
RAW_RING = 4
SPLIT_RING = 6


def gnn_kernel(nc, x, weights, bias_t, bias_rows, b1_row, edge_cols, edge_w, edge_rows, type_w, out):
    f32, f32r, bf16, i32 = (mybir.dt.float32, mybir.dt.float32r, mybir.dt.bfloat16, mybir.dt.int32)
    ALU = mybir.AluOpType
    ACT = mybir.ActivationFunctionType
    AX = mybir.AxisListType

    ctx = ExitStack()
    with ctx:
        def sb(name, shape, dt=f32):
            return ctx.enter_context(nc.sbuf_tensor(name, shape, dt))

        def sem(name):
            return ctx.enter_context(nc.semaphore(name))

        raw = sb("raw", [P, RAW_RING, CW])
        w_hi = sb("w_hi", [P, SPLIT_RING, CW], f32r)
        w_lo = sb("w_lo", [P, SPLIT_RING, CW], f32r)
        set_a, set_b, set_c = ((sb(f"{n}_hi", [P, KT, N], f32r), sb(f"{n}_lo", [P, KT, N], f32r))
                               for n in ("set_a", "set_b", "set_c"))
        parts_of = {"h": set_a, "v": set_a, "ag": set_a, "q": set_b, "attn": set_b, "ah3": set_b,
                    "k": set_c, "ah2": set_c}
        h_t = sb("h_t", [P, KT, N])
        z_t = sb("z_t", [P, KT, N])
        xa = sb("xa", [N, D])
        xb = sb("xb", [N, D])
        u = sb("u", [N, D])
        y_sb = sb("y_sb", [N, D])
        arena = sb("arena", [P, 4096])
        onehot = arena[:, :].bitcast(bf16)
        dst_oh = onehot[:, 0:2304].rearrange("p (c a n) -> p c a n", c=EC, a=2)
        src_oh = onehot[:, 2304:6912].rearrange("p (c a n) -> p c a n", c=EC, a=4)
        probs = arena[0:N, 0:1536].rearrange("p (h m) -> p h m", h=H)
        q2t = arena[:, 1536:2304].rearrange("p (k n) -> p k n", k=KT)
        k2t = arena[:, 2304:3072].rearrange("p (k n) -> p k n", k=KT)
        probs_t = arena[0:N, 1536:3072].rearrange("p (h m) -> p h m", h=H)
        v2 = arena[0:N, 3072:4096]
        b_l2 = arena[0:N, 0:D]
        b2_tile = arena[0:N, 3072:4096]

        bt = sb("bt", [P, 6, KT])
        b1 = sb("b1", [1, MID])
        ecol_i = sb("ecol_i", [P, 3, EC], i32)
        ecol = sb("ecol", [P, 3, EC])
        ew = sb("ew", [P, EC])
        ew_parts = sb("ew_parts", [P, 3, EC], bf16)
        ew_rest = sb("ew_rest", [P, 2, EC])
        erow_i = sb("erow_i", [2, E], i32)
        erow = y_sb[0:2, :].bitcast(bf16)[:, 0:E]
        coef = sb("coef", [2, P], bf16)
        cell = sb("cell", [P, EC])
        later = sb("later", [P, P], bf16)
        junk = z_t[:].rearrange("p k n -> p (k n)").bitcast(bf16)
        n_later = sb("n_later", [P, EC])
        digit = sb("digit", [P, EC])
        tw = sb("tw", [P, ETYPES])
        spa = sb("spa", [P, ETYPES])
        spb = sb("spb", [P, ETYPES])
        sp = sb("sp", [P, ETYPES])
        code = sb("code", [P, EC])
        vtmp = sb("vtmp", [P, EC])
        vtmp2 = sb("vtmp2", [P, EC])
        iota_i = sb("iota_i", [P, N], i32)
        iota = sb("iota", [P, N])
        ident = sb("ident", [P, P])
        ones = sb("ones", [P, N])
        eps_t = sb("eps_t", [P, 1])
        table = sb("table", [P, 1])
        stats = sb("stats", [N, 4, 4, 6])
        mv = sb("mv", [N, 4, 2])
        std = sb("std", [N, 4])
        rstd = sb("rstd", [N, 4])
        shift0 = sb("shift0", [N, 1])
        cnt = sb("cnt", [N, 2, N])
        deg = sb("deg", [N, 2])
        dsq = sb("dsq", [N, 2])
        dinv = sb("dinv", [N, 2])
        half_a = sb("half_a", [N, 2, N])
        a2t = sb("a2t", [N, N])
        a3t = sb("a3t", [N, N])
        a_s = sb("a_s", [N, N])
        a2_sum = sb("a2_sum", [N, 1])
        w96t = sb("w96t", [N, N])
        mask = sb("mask", [N, N])
        cls = sb("cls", [N, N])
        cls_i = sb("cls_i", [N, N], i32)
        mtmp = sb("mtmp", [N, N])
        nmx = sb("nmx", [N, H])
        sm = sb("sm", [N, H])
        rs = sb("rs", [N, H])
        u1t = sb("u1t", [N, N])
        hid = y_sb[:, 0:MID]

        ps = ctx.enter_context(nc.psum_tensor("ps", [P, 8, HALF], f32))

        def place(h):
            return 4 * (2 * (h // 8) + h % 2) + h % 8 // 2

        def y_ps(i):
            return ps[0:N, 2 * i:2 * i + 2, :]

        PARTS = [(0, 0, HALF), (1, HALF, HALF + MID), (2, HALF + MID, D)]

        def part_ps(i):
            bank, a, b = PARTS[i]
            return ps[0:N, bank, 0:b - a]

        raw_in = [sem(f"raw_in{i}") for i in range(RAW_RING)]
        hi_done = sem("hi_done")
        lo_done = sem("lo_done")
        chunk_used = sem("chunk_used")
        consts = sem("consts")
        S = {}

        def ev(name):
            if name not in S:
                S[name] = sem(name)
            return S[name]

        y_slot = {"q": 0, "k": 1, "v": 0, "iq": 1, "ik": 0, "iv": 1}
        block = ctx.enter_context(nc.Block())

        def raw_slot(c):
            return c % RAW_RING

        def wait_raw(eng, c):
            eng.wait_ge(raw_in[raw_slot(c)], 16 * (c // RAW_RING + 1))

        def split_index(c):
            return SPLIT.index(c)

        tr_order = ["q", "k", "v", "iq", "ik"]
        bias_of = {"q": 0, "k": 1, "v": 2, "iq": 3, "ik": 4}
        NCONST = 5 + EC

        @block.sync
        def _(sp_):
            sp_.dma_start(xa[:], x).then_inc(ev("x_in"), 16)
            sp_.dma_start(ecol_i[:], edge_cols).then_inc(ev("ecol_in"), 16)
            sp_.dma_start(erow_i[:], edge_rows).then_inc(ev("row_in"), 16)
            for c in range(NCHUNK):
                old = c - RAW_RING
                if old >= 0:
                    if old in WHOLE:
                        sp_.wait_ge(chunk_used, old + 1)
                    else:
                        sp_.wait_ge(lo_done, split_index(old) + 1)
                sp_.dma_start(raw[:, raw_slot(c), :], weights[c]).then_inc(raw_in[raw_slot(c)], 16)
                if c == 25:
                    sp_.wait_ge(ev("tr_h"), 2)
                    sp_.dma_start(u[:], bias_rows[0:1, :].partition_broadcast(N)).then_inc(ev("bo_in"), 16)
                if c == 27:
                    sp_.wait_ge(ev("tr_ik"), 2)
                    sp_.dma_start(y_sb[:], bias_rows[1:2, :].partition_broadcast(N)).then_inc(ev("l1b_in"), 16)
                if c == 29:
                    sp_.wait_ge(ev("probs_tr"), 4)
                    sp_.dma_start(b_l2, bias_rows[2:3, :].partition_broadcast(N)).then_inc(ev("l2b_in"), 16)
            sp_.wait_ge(ev("attn_mm"), 4)
            sp_.dma_start(b2_tile, bias_rows[3:4, :].partition_broadcast(N)).then_inc(ev("b2_in"), 16)
            sp_.wait_ge(ev("result"), 2)
            sp_.dma_start(out[:, 0:PARTS[2][1]], xb[:, 0:PARTS[2][1]]).then_inc(ev("stored0"), 16)
            sp_.wait_ge(ev("stored0"), 16)

        @block.gpsimd
        def _(pool):
            pool.iota(iota_i[:], pattern=[[1, N]], base=0, channel_multiplier=0).then_inc(consts, 1)
            pool.memset(ident[:], 0.0).then_inc(consts, 1)
            pool.memset(later[:], 1.0).then_inc(consts, 1)
            pool.wait_ge(consts, 3)
            pool.affine_select(out=ident[:], in_=ident[:], compare_op=ALU.not_equal, fill=1.0, base=0,
                               pattern=[[-1, P]], channel_multiplier=1).then_inc(consts, 1)
            pool.affine_select(out=later[:], in_=later[:], compare_op=ALU.is_gt, fill=0.0, base=0,
                               pattern=[[1, P]], channel_multiplier=-1).then_inc(consts, 1)
            pool.wait_ge(ev("row_in"), 16)
            pool.tensor_copy(erow, erow_i[:]).then_inc(ev("erow"), 1)
            for c in range(EC):
                pool.memset(digit[:, c:c + 1], 16.0 ** c).then_inc(consts, 1)

            pool.wait_ge(ev("ecol_f"), 1)
            step = ev("code_step")
            steps = [0]

            def chained(ins):
                steps[0] += 1
                ins.then_inc(step, 1)
                pool.wait_ge(step, steps[0])

            for t in range(ETYPES + 1):
                k = (t - 1) % ETYPES
                dst = code if t == 0 else vtmp
                chained(pool.tensor_scalar(dst[:], ecol[:, 2, :], float(t), 2.0 ** k, ALU.is_equal, ALU.mult))
                if t:
                    chained(pool.tensor_tensor(code[:], code[:], vtmp[:], ALU.add))
            pool.wait_ge(consts, NCONST)
            chained(pool.tensor_tensor(code[:], code[:], digit[:], ALU.mult))

            pool.wait_ge(ev("ew_in"), 16)
            chained(pool.tensor_copy(ew_parts[:, 0, :], ew[:]))
            chained(pool.tensor_tensor(ew_rest[:, 0, :], ew[:], ew_parts[:, 0, :], ALU.subtract))
            chained(pool.tensor_copy(ew_parts[:, 1, :], ew_rest[:, 0, :]))
            chained(pool.tensor_tensor(ew_rest[:, 1, :], ew_rest[:, 0, :], ew_parts[:, 1, :], ALU.subtract))
            chained(pool.tensor_copy(ew_parts[:, 2, :], ew_rest[:, 1, :]))
            pool.wait_ge(ev("onehots"), 2)
            for i in range(3):
                pool.tensor_tensor(src_oh[:, :, 1 + i, :], src_oh[:, :, 0, :],
                                   ew_parts[:, i, :].unsqueeze(2).broadcast_to((P, EC, N)),
                                   ALU.mult).then_inc(ev("edge_rows"), 1)
            pool.wait_ge(ev("last"), 1)
            chained(pool.tensor_tensor(code[:], code[:], n_later[:], ALU.mult))
            pool.tensor_tensor(dst_oh[:, :, 1, :], dst_oh[:, :, 0, :],
                               code[:].unsqueeze(2).broadcast_to((P, EC, N)), ALU.mult).then_inc(ev("edge_rows"), 1)
            pool.wait_ge(ev("present"), 1)
            pool.wait_ge(ev("classes"), 1)
            chained(pool.tensor_copy(cls[:], cls_i[:]))
            chained(pool.tensor_scalar(mask[:], mask[:], 1.0, NEG, ALU.subtract, ALU.mult))
            for j in range(ETYPES):
                k = (j + 1) % ETYPES
                chained(pool.tensor_scalar(mtmp[:], cls[:], float(j), sp[0:N, k:k + 1], ALU.is_equal, ALU.mult))
                last = pool.tensor_tensor(mask[:], mask[:], mtmp[:], ALU.add)
                if j < ETYPES - 1:
                    chained(last)
            last.then_inc(ev("mask"), 1)
            for b in range(4):
                pool.wait_ge(ev("row_sum"), b + 1)
                pool.tensor_tensor(probs[:, 4 * b:4 * b + 4, :], probs[:, 4 * b:4 * b + 4, :],
                                   rs[:, 4 * b:4 * b + 4].unsqueeze(2).broadcast_to((N, 4, N)),
                                   ALU.mult).then_inc(ev("normalized"), 1)
            pool.wait_ge(ev("bo_in"), 16)
            pool.tensor_tensor(xa[:], xa[:], u[:], ALU.add).then_inc(ev("x_bo"), 1)
            pool.wait_ge(ev("x_bo"), 1)
            pool.wait_ge(ev("l1b_in"), 16)
            pool.tensor_tensor(xb[:], xa[:], y_sb[:], ALU.add).then_inc(ev("x_bo_l1"), 1)
            pool.wait_ge(ev("l2b_in"), 16)
            pool.wait_ge(ev("a2_sum"), 1)
            pool.tensor_tensor(b_l2, b_l2, a2_sum[:].broadcast_to((N, D)), ALU.mult).then_inc(ev("l2b_rows"), 1)
            pool.wait_ge(ev("l2b_rows"), 1)
            pool.wait_ge(ev("x2"), 1)
            pool.tensor_tensor(xa[:], xb[:], b_l2, ALU.add).then_inc(ev("x2_b"), 1)
            pool.wait_ge(ev("b2_in"), 16)
            pool.wait_ge(ev("x3"), 1)
            pool.tensor_tensor(xb[:], xa[:], b2_tile, ALU.add).then_inc(ev("x3_b"), 1)

        @block.scalar
        def _(act):
            act.wait_ge(ev("eps"), 1)
            act.activation(table[:], eps_t[:], ACT.Sqrt).then_inc(ev("tables"), 1)
            act.dma_start(tw[:], type_w).then_inc(ev("tw_in"), 16)
            act.dma_start(ew[:], edge_w).then_inc(ev("ew_in"), 16)
            act.dma_start(bt[:], bias_t).then_inc(ev("bt_in"), 16)
            act.dma_start(b1[:], b1_row).then_inc(ev("b1_in"), 16)

            def split(c):
                if c in WHOLE:
                    return
                i = split_index(c)
                wait_raw(act, c)
                if i >= SPLIT_RING:
                    act.wait_ge(chunk_used, SPLIT[i - SPLIT_RING] + 1)
                act.activation(w_hi[:, i % SPLIT_RING, :], raw[:, raw_slot(c), :], ACT.Copy).then_inc(hi_done, 1)

            def evacuate(name):
                act.wait_ge(chunk_used, CPL * (LAYERS.index(name) + 1))
                i = tr_order.index(name)
                if i:
                    act.wait_ge(ev(f"tr_{tr_order[i - 1]}"), 2)
                for hf in range(2):
                    act.activation(y_sb[:, hf * HALF:(hf + 1) * HALF], y_ps(y_slot[name])[:, hf, :],
                                   ACT.Copy).then_inc(ev(f"y_{name}"), 1)

            def leading(name, src, per):
                for b in range(KT // per):
                    act.wait_ge(ev(f"{name}_t"), b + 1)
                    s = slice(per * b, per * b + per)
                    act.activation(parts_of[name][0][:, s, :], src[:, s, :], ACT.Copy).then_inc(ev(f"{name}_h"), 1)

            def leading_ps(name, tiles, per):
                for b in range(tiles // per):
                    act.wait_ge(ev(f"{name}_mm"), b + 1)
                    act.activation(parts_of[name][0][:, per * b:per * (b + 1), :],
                                   ps[:, 4 + b, 0:per * N].rearrange("p (k n) -> p k n", k=per),
                                   ACT.Copy).then_inc(ev(f"{name}_h"), 1)

            def root(i):
                act.wait_ge(ev(f"mv{i}"), 1)
                act.activation(std[:, i:i + 1], mv[:, i, 1:2], ACT.Sqrt, bias=eps_t[0:N, :]).then_inc(ev(f"std{i}"), 1)

            root(0)
            act.wait_ge(ev("shift0"), 1)
            for hf in range(2):
                s = slice(hf * HALF, (hf + 1) * HALF)
                act.activation(u[:, s], xa[:, s], ACT.Relu, bias=shift0[:], scale=rstd[:, 0:1]).then_inc(ev("h0"), 1)
            leading("h", h_t, 4)
            split(2)
            split(3)
            act.wait_ge(ev("neg_abs"), 1)
            act.activation(spb[:], spa[:], ACT.Exp).then_inc(ev("sp_exp"), 1)
            act.wait_ge(ev("sp_exp"), 1)
            act.activation(sp[:], spb[:], ACT.Ln, bias=1.0).then_inc(ev("sp_ln"), 1)
            split(5)
            split(6)
            evacuate("q")
            split(7)
            leading("q", z_t, 4)
            split(8)
            split(9)
            split(10)
            evacuate("k")
            split(11)
            leading("k", z_t, 4)
            for c in range(12, 15):
                split(c)
            evacuate("v")
            split(15)
            act.wait_ge(ev("deg"), 2)
            act.activation(dsq[:], deg[:], ACT.Sqrt).then_inc(ev("dsq"), 1)
            act.wait_ge(ev("tables"), 1)
            act.activation(table[:], eps_t[:], ACT.Exp).then_inc(ev("tables"), 1)
            act.wait_ge(chunk_used, 3 * CPL)
            leading("v", z_t, 4)
            for c in range(16, 19):
                split(c)
            evacuate("iq")
            for c in range(19, 23):
                split(c)
            evacuate("ik")
            split(23)
            for b in range(4):
                act.wait_ge(ev("row_max"), b + 1)
                for k in range(4):
                    h = 4 * b + k
                    last = act.activation(probs[:, h, :], probs[:, h, :], ACT.Exp, bias=nmx[:, h:h + 1], scale=-1.0,
                                          accum_out=sm[:, h:h + 1])
                last.then_inc(ev("exps"), 1)
            split(24)
            act.wait_ge(ev("tables"), 2)
            act.activation(table[:], eps_t[:], ACT.Sqrt).then_inc(ev("tables"), 1)
            split(25)
            act.wait_ge(ev("iv_half"), 1)
            act.activation(v2[:, 0:HALF], y_ps(y_slot["iv"])[:, 0, :], ACT.Copy).then_inc(ev("v2a"), 1)
            for b in range(4):
                act.wait_ge(ev("probs_tr"), b + 1)
                act.activation(probs_t[:, 4 * b:4 * b + 4, :], ps[0:N, 4 + b, 0:4 * N].rearrange("p (h m) -> p h m", h=4),
                               ACT.Copy).then_inc(ev("probs_t"), 1)
            leading("attn", z_t, 2)
            for c in range(26, 30):
                split(c)
            root(1)
            split(30)
            root(2)
            split(31)
            leading_ps("ah2", KT, 2)
            split(32)
            split(33)
            root(3)
            leading_ps("ah3", KT, 2)
            act.wait_ge(ev("hid_mm"), 1)
            act.activation(hid, ps[0:N, 3, 0:MID], ACT.Relu).then_inc(ev("hid"), 1)
            leading_ps("ag", 2, 1)
            act.wait_ge(ev("result"), 3)
            act.dma_start(out[:, PARTS[2][1]:D], xb[:, PARTS[2][1]:D]).then_inc(ev("stored1"), 16)
            act.wait_ge(ev("stored1"), 16)

        @block.vector
        def _(dve):
            done = sem("dve_chain")
            chain = [0]

            def link(ins):
                chain[0] += 1
                ins.then_inc(done, 1)
                dve.wait_ge(done, chain[0])

            def split(c):
                if c in WHOLE:
                    return
                i = split_index(c)
                dve.wait_ge(hi_done, i + 1)
                dve.tensor_tensor(w_lo[:, i % SPLIT_RING, :], raw[:, raw_slot(c), :],
                                  w_hi[:, i % SPLIT_RING, :].bitcast(f32), ALU.subtract).then_inc(lo_done, 1)

            def add_bias(name, dst, banks):
                for b in range(2):
                    dve.wait_ge(ev(f"tr_{name}"), b + 1)
                    dve.tensor_tensor(dst[:, 4 * b:4 * b + 4, :],
                                      ps[:, banks[b], 0:4 * N].rearrange("p (k n) -> p k n", k=4),
                                      bt[:, bias_of[name], 4 * b:4 * b + 4].unsqueeze(2).broadcast_to((P, 4, N)),
                                      ALU.add).then_inc(ev(f"{name}_t"), 1)

            def rest(name, src, per, blocks):
                for b in blocks:
                    dve.wait_ge(ev(f"{name}_h"), b + 1)
                    s = slice(per * b, per * b + per)
                    hi, lo = parts_of[name]
                    dve.tensor_tensor(lo[:, s, :], src[:, s, :], hi[:, s, :].bitcast(f32),
                                      ALU.subtract).then_inc(ev(f"{name}_l"), 1)

            def rest_ps(name, tiles, per):
                for b in range(tiles // per):
                    s = slice(per * b, per * (b + 1))
                    hi, lo = parts_of[name]
                    dve.wait_ge(ev(f"{name}_h"), b + 1)
                    dve.tensor_tensor(lo[:, s, :], ps[:, 4 + b, 0:per * N].rearrange("p (k n) -> p k n", k=per),
                                      hi[:, s, :].bitcast(f32), ALU.subtract).then_inc(ev(f"{name}_l"), 1)

            def bn(i, seg, xt, a, b):
                return dve.bn_stats(stats[:, i, seg, :], xt[:, a:b])

            def aggregate(i, nseg):
                dve.bn_aggr(mv[:, i, :], stats[:, i, 0:nseg, :]).then_inc(ev(f"mv{i}"), 1)

            def reciprocal_std(i):
                dve.wait_ge(ev(f"std{i}"), 1)
                link(dve.reciprocal(rstd[:, i:i + 1], std[:, i:i + 1]))

            dve.memset(eps_t[:], EPS).then_inc(ev("eps"), 1)
            dve.memset(ones[:], 1.0).then_inc(ev("ones"), 1)
            link(dve.memset(coef[:], 1.0))
            dve.memset(coef[0:1, :], float(N)).then_inc(ev("coef"), 1)
            dve.wait_ge(ev("x_in"), 16)
            link(bn(0, 0, xa, 0, HALF))
            link(bn(0, 1, xa, HALF, D))
            aggregate(0, 2)
            dve.wait_ge(consts, 1)
            link(dve.tensor_copy(iota[:], iota_i[:]))
            reciprocal_std(0)
            dve.wait_ge(ev("mv0"), 1)
            dve.tensor_scalar(shift0[:], mv[:, 0, 0:1], rstd[:, 0:1], -1.0, ALU.mult, ALU.mult).then_inc(ev("shift0"), 1)
            dve.wait_ge(ev("ecol_in"), 16)
            dve.tensor_copy(ecol[:], ecol_i[:]).then_inc(ev("ecol_f"), 1)
            dve.wait_ge(ev("ecol_f"), 1)

            def one_hots(oh, k):
                dve.tensor_tensor(oh[:, :, 0, :], iota[:].unsqueeze(1).broadcast_to((P, EC, N)),
                                  ecol[:, k, :].unsqueeze(2).broadcast_to((P, EC, N)),
                                  ALU.is_equal).then_inc(ev("onehots"), 1)

            one_hots(src_oh, 0)
            for b in range(2):
                dve.wait_ge(ev("tr_h"), b + 1)
                dve.tensor_copy(h_t[:, 4 * b:4 * b + 4, :],
                                ps[:, 2 + b, 0:4 * N].rearrange("p (k n) -> p k n", k=4)).then_inc(ev("h_t"), 1)
            rest("h", h_t, 4, range(2))
            one_hots(dst_oh, 1)
            dve.wait_ge(ev("tw_in"), 16)
            link(dve.tensor_scalar(spa[:], tw[:], -1.0, None, ALU.mult))
            dve.tensor_tensor(spa[:], spa[:], tw[:], ALU.min).then_inc(ev("neg_abs"), 1)
            link(dve.tensor_scalar(vtmp2[:], ecol[:, 0, :], float(N), None, ALU.mult))
            link(dve.tensor_tensor(cell[:], vtmp2[:], ecol[:, 1, :], ALU.add))
            dve.wait_ge(ev("cells"), 1)
            dve.wait_ge(consts, NCONST)
            cells_ps = ps[:, 5:8, :].rearrange("p b n -> p (b n)")
            for c in range(EC):
                s = slice(P * c, P * c + P)
                dve.scalar_tensor_tensor(out=junk[:, s], in0=cells_ps[:, s], scalar=cell[:, c:c + 1], in1=later[:],
                                         op0=ALU.is_equal, op1=ALU.mult, accum_out=n_later[:, c:c + 1])\
                   .then_inc(ev("counted"), 1)
                if c == 5:
                    split(2)
            dve.wait_ge(ev("counted"), EC)
            dve.tensor_scalar(n_later[:], n_later[:], 0.0, None, ALU.is_equal).then_inc(ev("last"), 1)
            for c in range(3, 8):
                split(c)
            dve.wait_ge(ev("bt_in"), 16)
            add_bias("q", z_t, (4, 7))
            split(8)
            rest("q", z_t, 4, range(2))
            dve.wait_ge(ev("sp_ln"), 1)
            link(dve.tensor_scalar(spa[:], tw[:], 0.0, None, ALU.max))
            link(dve.tensor_tensor(sp[:], sp[:], spa[:], ALU.add))
            split(9)
            split(10)
            dve.wait_ge(ev("graph_mm"), 2)
            dve.tensor_tensor(cnt[:, 0, :], ps[0:N, 5, 0:N], ident[0:N, 0:N], ALU.add).then_inc(ev("cnt0"), 1)
            link(dve.scalar_tensor_tensor(out=cls[:], in0=ident[0:N, 0:N], scalar=0.5, in1=ps[0:N, 5, N:2 * N],
                                          op0=ALU.mult, op1=ALU.max))
            dve.tensor_scalar(mask[:], cls[:], 0.0, None, ALU.is_gt).then_inc(ev("present"), 1)
            dve.tensor_scalar(cls_i[:], cls[:].bitcast(i32), 23, 3, ALU.logical_shift_right, ALU.bitwise_and)\
               .then_inc(ev("classes"), 1)
            dve.tensor_copy(w96t[:], ps[0:N, 6, 0:N]).then_inc(ev("w96t"), 1)
            dve.wait_ge(ev("cnt0"), 1)
            dve.tensor_reduce(deg[:, 0:1], cnt[:, 0, :], AX.X, ALU.add).then_inc(ev("deg"), 1)
            split(11)
            add_bias("k", z_t, (4, 7))
            split(12)
            rest("k", z_t, 4, range(2))
            split(13)
            dve.wait_ge(ev("cnt_tr"), 1)
            link(dve.tensor_copy(cnt[:, 1, :], ps[0:N, 5, 2 * N:3 * N]))
            dve.tensor_reduce(deg[:, 1:2], cnt[:, 1, :], AX.X, ALU.add).then_inc(ev("deg"), 1)
            split(14)
            split(15)
            add_bias("v", z_t, (4, 7))
            split(16)
            rest("v", z_t, 4, range(2))
            dve.wait_ge(ev("dsq"), 1)
            link(dve.reciprocal(dinv[:], dsq[:]))
            for i in range(2):
                dve.tensor_scalar(half_a[:, i, :], cnt[:, i, :], dinv[:, i:i + 1], None,
                                  ALU.mult).then_inc(ev("half_a"), 1)
            for c in range(17, 20):
                split(c)
            add_bias("iq", q2t, (4, 5))
            split(20)
            dve.wait_ge(ev("half_tr"), 2)
            dve.tensor_scalar(a2t[:], ps[0:N, 7, 0:N], dinv[:, 0:1], None, ALU.mult).then_inc(ev("adjacency"), 1)
            dve.tensor_scalar(a3t[:], ps[0:N, 7, N:2 * N], dinv[:, 1:2], None, ALU.mult).then_inc(ev("adjacency"), 1)
            split(21)
            split(22)
            add_bias("ik", k2t, (6, 7))
            dve.wait_ge(ev("mask"), 1)

            for b in range(4):
                s = slice(4 * b, 4 * b + 4)
                dve.wait_ge(ev("scores"), b + 1)
                link(dve.scalar_tensor_tensor(out=probs[:, s, :],
                                              in0=ps[0:N, 4 + b, 0:4 * N].rearrange("p (h m) -> p h m", h=4),
                                              scalar=-SCALE, in1=mask[:].unsqueeze(1).broadcast_to((N, 4, N)),
                                              op0=ALU.mult, op1=ALU.subtract))
                dve.tensor_reduce(nmx[:, s], probs[:, s, :], AX.X, ALU.min).then_inc(ev("row_max"), 1)
            split(23)
            for b in range(4):
                s = slice(4 * b, 4 * b + 4)
                dve.wait_ge(ev("exps"), b + 1)
                dve.reciprocal(rs[:, s], sm[:, s]).then_inc(ev("row_sum"), 1)
            split(24)

            split(25)
            dve.wait_ge(ev("iv_half"), 2)
            dve.tensor_copy(v2[:, HALF:D], y_ps(y_slot["iv"])[:, 1, :]).then_inc(ev("v2b"), 1)
            for b in range(4):
                s = slice(2 * b, 2 * b + 2)
                dve.wait_ge(ev("attn_mm"), b + 1)
                dve.tensor_tensor(z_t[:, s, :], ps[:, 4 + b, 0:2 * N].rearrange("p (k n) -> p k n", k=2),
                                  bt[:, 5, s].unsqueeze(2).broadcast_to((P, 2, N)), ALU.add).then_inc(ev("attn_t"), 1)
                if b:
                    rest("attn", z_t, 2, [b - 1])
            rest("attn", z_t, 2, [3])
            split(26)
            split(27)
            dve.wait_ge(ev("row_mm"), 1)
            dve.tensor_copy(a2_sum[:], ps[0:N, 3, 0:1]).then_inc(ev("a2_sum"), 1)
            split(28)

            SL = [slice(a, b) for _, a, b in PARTS]

            def residual(dst, i):
                return dve.tensor_tensor(dst[:, SL[i]], part_ps(i), dst[:, SL[i]], ALU.add)

            dve.wait_ge(ev("x_bo_l1"), 1)
            for i in range(2):
                dve.wait_ge(ev("o_part"), i + 1)
                link(residual(xa, i))
                link(bn(1, i, xa, PARTS[i][1], PARTS[i][2]))
                link(residual(xb, i))
                link(bn(2, i, xb, max(PARTS[i][1], N), PARTS[i][2]))
            dve.wait_ge(ev("o_part"), 3)
            link(residual(xa, 2))
            link(bn(1, 2, xa, PARTS[2][1], D))
            aggregate(1, 3)
            dve.wait_ge(ev("mv1"), 1)
            dve.tensor_scalar(u[:, 0:N], xa[:, 0:N], mv[:, 1, 0:1], 0.0, ALU.subtract, ALU.max).then_inc(ev("u1"), 1)
            link(residual(xb, 2))
            dve.wait_ge(ev("tr_u1"), 1)
            dve.tensor_copy(u1t[:], ps[0:N, 4, 0:N]).then_inc(ev("u1t"), 1)
            link(bn(2, 2, xb, PARTS[2][1], D))
            reciprocal_std(1)
            dve.wait_ge(ev("l1_mm"), 1)
            dve.scalar_tensor_tensor(out=xb[:, 0:N], in0=ps[0:N, 5, 0:N], scalar=rstd[:, 1:2], in1=xb[:, 0:N],
                                     op0=ALU.mult, op1=ALU.add).then_inc(ev("x2"), 1)
            dve.wait_ge(ev("x2"), 1)
            link(bn(2, 3, xb, 0, N))

            def norm_and_scale(i, nseg, xt, at, key):
                aggregate(i, nseg)
                dve.wait_ge(ev(f"mv{i}"), 1)
                for hf in range(2):
                    s = slice(hf * HALF, (hf + 1) * HALF)
                    if hf:
                        reciprocal_std(i)
                        dve.tensor_scalar(a_s[:], at[:], rstd[:, i:i + 1], None, ALU.mult).then_inc(ev(f"as_{key}"), 1)
                    dve.tensor_scalar(u[:, s], xt[:, s], mv[:, i, 0:1], 0.0, ALU.subtract, ALU.max)\
                       .then_inc(ev(f"u_{key}"), 1)

            norm_and_scale(2, 4, xb, a2t, "ah2")
            rest_ps("ah2", KT, 2)
            for c in range(29, 33):
                split(c)
            split(33)
            dve.wait_ge(ev("x2_b"), 1)
            for i in range(3):
                dve.wait_ge(ev("W_part"), i + 1)
                ins = residual(xa, i)
                if i == 2:
                    ins.then_inc(ev("x3"), 1)
                    dve.wait_ge(ev("x3"), 1)
                else:
                    link(ins)
                link(bn(3, i, xa, PARTS[i][1], PARTS[i][2]))
            norm_and_scale(3, 3, xa, a3t, "ah3")
            rest_ps("ah3", KT, 2)
            rest_ps("ag", 2, 1)
            dve.wait_ge(ev("x3_b"), 1)
            for i in range(3):
                dve.wait_ge(ev("W2_part"), i + 1)
                residual(xb, i).then_inc(ev("result"), 1)

        @block.tensor
        def _(pe):
            def mm(o, l, r, start, stop):
                return pe.matmul(o, l, r, start=start, stop=stop)

            def operands(c, z):
                if c in WHOLE:
                    assert z == "h"
                    wait_raw(pe, c)
                    return [(h_t, raw[:, raw_slot(c), :].rearrange("p (t n) -> p t n", t=TPC))]
                i = split_index(c)
                pe.wait_ge(lo_done, i + 1)
                hi = w_hi[:, i % SPLIT_RING, :].rearrange("p (t n) -> p t n", t=TPC)
                lo = w_lo[:, i % SPLIT_RING, :].rearrange("p (t n) -> p t n", t=TPC)
                zh, zl = parts_of[z]
                return [(zh, hi), (zh, lo), (zl, hi)]

            def chunk(name, c, z, tiles=range(TPC)):
                pairs = operands(c, z)
                for t in tiles:
                    kt = TPC * (c % CPL) + t
                    for pi, (zp, w) in enumerate(pairs):
                        for hf in range(2):
                            last = mm(y_ps(y_slot[name])[:, hf, :], zp[:, kt, :], w[:, t, hf * HALF:(hf + 1) * HALF],
                                      kt == 0 and pi == 0, kt == KT - 1 and pi == len(pairs) - 1)
                if TPC - 1 in tiles:
                    last.then_inc(chunk_used, 1)

            def last_chunks(chunks, kt0, z, outs, part_done, first=False):
                pairs = [operands(c, z) for c in chunks]
                for oi, (acc, a, b) in enumerate(outs):
                    for ci, c in enumerate(chunks):
                        for t in range(TPC):
                            kt = kt0 + TPC * ci + t
                            for pi, (zp, w) in enumerate(pairs[ci]):
                                stop = c == chunks[-1] and t == TPC - 1 and pi == len(pairs[ci]) - 1
                                last = mm(acc, zp[:, kt, :], w[:, t, a:b], first and ci == 0 and t == 0 and pi == 0, stop)
                        if oi == len(outs) - 1 and c != chunks[-1]:
                            last.then_inc(chunk_used, 1)
                    last.then_inc(part_done, 1)
                pe.wait_ge(part_done, len(outs))
                pe.nop().then_inc(chunk_used, 1)

            def transposes(name, banks):
                for b in range(2):
                    pe.wait_ge(ev(f"y_{name}"), b + 1)
                    for k in range(4):
                        kt = 4 * b + k
                        last = pe.transpose(ps[:, banks[b], k * N:(k + 1) * N], y_sb[:, kt * P:(kt + 1) * P],
                                            ident[0:N, 0:N])
                    last.then_inc(ev(f"tr_{name}"), 1)

            pe.wait_ge(ev("coef"), 1)
            pe.wait_ge(ev("erow"), 1)
            for b in range(3):
                last = mm(ps[:, 5 + b, :], coef[:], erow[:, b * HALF:(b + 1) * HALF], True, True)
            last.then_inc(ev("cells"), 1)
            pe.wait_ge(consts, 5)
            for b in range(2):
                pe.wait_ge(ev("h0"), b + 1)
                for k in range(4):
                    kt = 4 * b + k
                    last = pe.transpose(ps[:, 2 + b, k * N:(k + 1) * N], u[:, kt * P:(kt + 1) * P], ident[0:N, 0:N])
                last.then_inc(ev("tr_h"), 1)

            pe.wait_ge(ev("h_t"), 2)
            chunk("q", 0, "h")
            pe.wait_ge(ev("h_l"), 2)
            for c in range(1, 4):
                chunk("q", c, "h")
            chunk("k", 4, "h")
            transposes("q", (4, 7))
            for c in range(5, 8):
                chunk("k", c, "h")
            pe.wait_ge(ev("edge_rows"), 4)
            for c in range(EC):
                last = mm(ps[0:N, 5, 0:2 * N], src_oh[:, c, 0, :], dst_oh[:, c, :, :].rearrange("p a n -> p (a n)"),
                          c == 0, c == EC - 1)
            last.then_inc(ev("graph_mm"), 1)
            for c in range(EC):
                for i in range(3):
                    last = mm(ps[0:N, 6, 0:N], dst_oh[:, c, 0, :], src_oh[:, c, 1 + i, :],
                              c == 0 and i == 0, c == EC - 1 and i == 2)
            last.then_inc(ev("graph_mm"), 1)
            pe.wait_ge(ev("y_q"), 2)
            chunk("v", 8, "h")
            pe.wait_ge(ev("q_t"), 2)
            transposes("k", (4, 7))
            for c in range(9, 12):
                chunk("v", c, "h")
            pe.wait_ge(ev("q_l"), 2)
            pe.wait_ge(ev("y_k"), 2)
            chunk("iq", 12, "q")
            pe.wait_ge(ev("cnt0"), 1)
            pe.transpose(ps[0:N, 5, 2 * N:3 * N], cnt[:, 0, :], ident[0:N, 0:N]).then_inc(ev("cnt_tr"), 1)
            pe.wait_ge(ev("k_t"), 2)
            transposes("v", (4, 7))
            for c in range(13, 16):
                chunk("iq", c, "q")
            pe.wait_ge(ev("k_l"), 2)
            pe.wait_ge(ev("y_v"), 2)
            chunk("ik", 16, "k")
            pe.wait_ge(ev("v_t"), 2)
            pe.wait_ge(ev("deg"), 2)
            transposes("iq", (4, 5))
            chunk("ik", 17, "k")
            pe.wait_ge(ev("half_a"), 2)
            for i in range(2):
                pe.transpose(ps[0:N, 7, i * N:(i + 1) * N], half_a[:, i, :], ident[0:N, 0:N]).then_inc(ev("half_tr"), 1)
            for c in range(18, 20):
                chunk("ik", c, "k")
            pe.wait_ge(ev("v_l"), 2)
            pe.wait_ge(ev("y_iq"), 2)
            chunk("iv", 20, "v", (0,))
            pe.wait_ge(ev("w96t"), 1)
            pe.wait_ge(ev("adjacency"), 2)
            transposes("ik", (6, 7))
            chunk("iv", 20, "v", (1,))
            pe.wait_ge(ev("iq_t"), 2)
            pe.wait_ge(ev("ik_t"), 2)
            for pair in range(2):
                for k in range(4):
                    for odd in range(2):
                        kt = 4 * pair + k
                        r = slice(DH * odd, DH * odd + DH)
                        last = mm(ps[0:N, 4 + 2 * pair + odd, k * N:(k + 1) * N], q2t[r, kt, :], k2t[r, kt, :], True, True)
                        if k == 3:
                            last.then_inc(ev("scores"), 1)
            chunk("iv", 21, "v")
            last_chunks([22, 23], 4, "v", [(y_ps(1)[:, hf, :], hf * HALF, (hf + 1) * HALF) for hf in range(2)],
                        ev("iv_half"))
            for b in range(4):
                pe.wait_ge(ev("normalized"), b + 1)
                for k in range(4):
                    last = pe.transpose(ps[0:N, 4 + b, k * N:(k + 1) * N], probs[:, 4 * b + k, :], ident[0:N, 0:N])
                last.then_inc(ev("probs_tr"), 1)
            for b in range(4):
                pe.wait_ge(ev("v2b" if b >= 2 else "v2a"), 1)
                pe.wait_ge(ev("probs_t"), 2 * (b // 2) + 2)
                for k in range(4):
                    h = 4 * b + k
                    r = slice(DH * (h % 2), DH * (h % 2) + DH)
                    c0 = (k // 2) * N
                    last = mm(ps[r, 4 + b, c0:c0 + N], v2[:, h * DH:(h + 1) * DH], probs_t[:, place(h), :], True, True)
                last.then_inc(ev("attn_mm"), 1)

            def residual_layer(c0, z, blocks, part_done):
                for ci in range(CPL - 2):
                    pe.wait_ge(blocks, ci + 1)
                    pairs = operands(c0 + ci, z)
                    for t in range(TPC):
                        kt = TPC * ci + t
                        for pi, (zp, w) in enumerate(pairs):
                            for i, (_, a, b) in enumerate(PARTS):
                                last = mm(part_ps(i), zp[:, kt, :], w[:, t, a:b], kt == 0 and pi == 0, False)
                    last.then_inc(chunk_used, 1)
                pe.wait_ge(blocks, CPL)
                last_chunks([c0 + 2, c0 + 3], 4, z, [(part_ps(i), a, b) for i, (_, a, b) in enumerate(PARTS)], part_done)

            pe.wait_ge(ev("ones"), 1)
            mm(ps[0:N, 3, 0:1], a2t[:], ones[0:N, 0:1], True, True).then_inc(ev("row_mm"), 1)
            residual_layer(6 * CPL, "attn", ev("attn_l"), ev("o_part"))
            pe.wait_ge(ev("u1"), 1)
            pe.transpose(ps[0:N, 4, 0:N], u[:, 0:N], ident[0:N, 0:N]).then_inc(ev("tr_u1"), 1)
            pe.wait_ge(ev("u1t"), 1)
            mm(ps[0:N, 5, 0:N], u1t[:], w96t[:], True, True).then_inc(ev("l1_mm"), 1)

            def aggregation(key):
                pe.wait_ge(ev(f"as_{key}"), 1)
                for b in range(4):
                    pe.wait_ge(ev(f"u_{key}"), b // 2 + 1)
                    for k in range(2):
                        kt = 2 * b + k
                        last = mm(ps[:, 4 + b, k * N:(k + 1) * N], u[:, kt * P:(kt + 1) * P], a_s[:], True, True)
                    last.then_inc(ev(f"{key}_mm"), 1)

            aggregation("ah2")
            residual_layer(7 * CPL, "ah2", ev("ah2_l"), ev("W_part"))
            pe.wait_ge(ev("b1_in"), 16)
            mm(ps[0:N, 3, 0:MID], ones[0:1, :], b1[:], True, False)
            aggregation("ah3")
            i = split_index(C_W1)
            pe.wait_ge(lo_done, i + 1)
            hi_z, lo_z = parts_of["ah3"]
            for kt in range(KT):
                if kt % 2 == 0:
                    pe.wait_ge(ev("ah3_l"), kt // 2 + 1)
                s = slice(kt * MID, (kt + 1) * MID)
                hi, lo = w_hi[:, i % SPLIT_RING, s], w_lo[:, i % SPLIT_RING, s]
                mm(ps[0:N, 3, 0:MID], hi_z[:, kt, :], hi, False, False)
                mm(ps[0:N, 3, 0:MID], hi_z[:, kt, :], lo, False, False)
                last = mm(ps[0:N, 3, 0:MID], lo_z[:, kt, :], hi, False, kt == KT - 1)
            last.then_inc(ev("hid_mm"), 1)
            pe.wait_ge(ev("hid"), 1)
            for k in range(2):
                mm(ps[:, 4 + k, 0:N], hid[:, k * P:(k + 1) * P], a3t[:], True, True).then_inc(ev("ag_mm"), 1)
            pe.wait_ge(ev("ag_l"), 2)
            last_chunks([C_W2], 0, "ag", [(part_ps(i), a, b) for i, (_, a, b) in enumerate(PARTS)], ev("W2_part"), first=True)


def kernel(**inputs):
    import numpy as np
    import concourse.bacc as bacc
    from concourse.bass_utils import run_bass_kernel_spmd

    a = {k: np.asarray(v) for k, v in inputs.items()}

    def chunks(w_kn):
        k, n = w_kn.shape
        return w_kn.reshape(k // (TPC * P), TPC, P, n).transpose(0, 2, 1, 3).reshape(-1, P, TPC * n)

    full = ["L0_gnn_wq", "L0_gnn_wk", "L0_gnn_wv", "L0_gnn_wiq", "L0_gnn_wik", "L0_gnn_wiv", "L0_gnn_wo", "L2_gnn_W"]
    w1 = a["L3_gnn_W1"].reshape(KT, P, MID).transpose(1, 0, 2).reshape(1, P, CW)
    weights = np.ascontiguousarray(np.concatenate([chunks(a[n].T) for n in full] + [w1, chunks(a["L3_gnn_W2"])]))
    cols = ["L0_gnn_bq", "L0_gnn_bk", "L0_gnn_bv", "L0_gnn_biq", "L0_gnn_bik", "L0_gnn_biv"]
    bias_t = np.ascontiguousarray(np.stack([a[n].reshape(KT, P).T for n in cols], axis=1))
    bias_rows = np.stack([a[n] for n in ("L0_gnn_bo", "L1_gnn_bias", "L2_gnn_b", "L3_gnn_b2")])
    edge_cols = np.ascontiguousarray(np.stack([a[n].reshape(EC, P).T for n in ("src", "dst", "edge_type_5")], axis=1))
    arrays = {
        "x": a["x"], "weights": weights, "bias_t": bias_t, "bias_rows": bias_rows, "b1_row": a["L3_gnn_b1"].reshape(1, MID), "edge_cols": edge_cols,
        "edge_w": np.ascontiguousarray(a["edge_weight"].reshape(EC, P).T),
        "edge_rows": np.ascontiguousarray(np.stack([a["src"], a["dst"]])),
        "type_w": np.ascontiguousarray(np.broadcast_to(a["L0_gnn_edge_type_weights"], (P, ETYPES))),
    }
    nc = bacc.Bacc("TRN2", target_bir_lowering=False, num_devices=1)
    aps = [nc.dram_tensor(n, v.shape, mybir.dt.from_np(v.dtype), kind="ExternalInput").ap() for n, v in arrays.items()]
    out = nc.dram_tensor("out", (N, D), mybir.dt.float32, kind="ExternalOutput").ap()
    gnn_kernel(nc, *aps, out)
    r = run_bass_kernel_spmd(nc, [arrays], core_ids=[0])
    return r.results[0]["out"]
```

```python
from contextlib import ExitStack

import concourse.bass as bass
from concourse import mybir

N = 96
D = 1024
H = 16
DH = D // H
MID = 256
E = 1536
P = 128
KT = D // P
EC = E // P
HALF = 512
ETYPES = 4
EPS = 1e-5
SCALE = DH ** -0.5
NEG = 1.0e30

TPC = 2
CW = TPC * D
LAYERS = ["q", "k", "v", "iq", "ik", "iv", "o", "W"]
CPL = KT // TPC
C_W1 = len(LAYERS) * CPL
C_W2 = C_W1 + 1
NCHUNK = C_W2 + 1
WHOLE = {0, 1, 2, 22}
SPLIT = [c for c in range(NCHUNK) if c not in WHOLE]
RAW_RING = 6
SPLIT_RING = 5
WARM_UP = 12
KEEP_BUSY = (8, 8, 8)


def gnn_kernel(nc, x, weights, bias_t, bias_rows, b1_row, edge_cols, edge_w, edge_rows, type_w, out):
    f32, f32r, bf16, i32 = (mybir.dt.float32, mybir.dt.float32r, mybir.dt.bfloat16, mybir.dt.int32)
    ALU = mybir.AluOpType
    ACT = mybir.ActivationFunctionType
    AX = mybir.AxisListType

    ctx = ExitStack()
    with ctx:
        def sb(name, shape, dt=f32):
            return ctx.enter_context(nc.sbuf_tensor(name, shape, dt))

        def sem(name):
            return ctx.enter_context(nc.semaphore(name))

        raw = sb("raw", [P, RAW_RING, CW])
        w_hi = sb("w_hi", [P, SPLIT_RING, CW], f32r)
        w_lo = sb("w_lo", [P, SPLIT_RING, CW], f32r)
        set_a, set_b, set_c = ((sb(f"{n}_hi", [P, KT, N], f32r), sb(f"{n}_lo", [P, KT, N], f32r))
                               for n in ("set_a", "set_b", "set_c"))
        parts_of = {"h": set_a, "v": set_a, "ag": set_a, "q": set_b, "attn": set_b, "ah3": set_b,
                    "k": set_c, "ah2": set_c}
        h_t = sb("h_t", [P, KT, N])
        z_t = sb("z_t", [P, KT, N])
        xa = sb("xa", [N, D])
        xb = sb("xb", [N, D])
        u = sb("u", [N, D])
        y_sb = sb("y_sb", [N, D])
        arena = sb("arena", [P, 4096])
        onehot = arena[:, :].bitcast(bf16)
        dst_oh = onehot[:, 0:2304].rearrange("p (c a n) -> p c a n", c=EC, a=2)
        src_oh = onehot[:, 2304:6912].rearrange("p (c a n) -> p c a n", c=EC, a=4)
        probs = arena[0:N, 0:1536].rearrange("p (h m) -> p h m", h=H)
        q2t = arena[:, 1536:2304].rearrange("p (k n) -> p k n", k=KT)
        k2t = arena[:, 2304:3072].rearrange("p (k n) -> p k n", k=KT)
        probs_t = arena[0:N, 1536:3072].rearrange("p (h m) -> p h m", h=H)
        v2 = arena[0:N, 3072:4096]
        b_l2 = arena[0:N, 0:D]
        b2_tile = arena[0:N, 3072:4096]

        bt = sb("bt", [P, 6, KT])
        b1 = sb("b1", [1, MID])
        ecol_i = sb("ecol_i", [P, 3, EC], i32)
        ecol = sb("ecol", [P, 3, EC])
        ew = sb("ew", [P, EC])
        ew_parts = sb("ew_parts", [P, 3, EC], bf16)
        ew_rest = sb("ew_rest", [P, 2, EC])
        erow_i = sb("erow_i", [2, E], i32)
        erow = y_sb[0:2, :].bitcast(bf16)[:, 0:E]
        coef = sb("coef", [2, P], bf16)
        cell = sb("cell", [P, EC])
        later = sb("later", [P, P], bf16)
        junk = z_t[:].rearrange("p k n -> p (k n)").bitcast(bf16)
        n_later = sb("n_later", [P, EC])
        digit = sb("digit", [P, EC])
        tw = sb("tw", [P, ETYPES])
        spa = sb("spa", [P, ETYPES])
        spb = sb("spb", [P, ETYPES])
        sp = sb("sp", [P, ETYPES])
        code = sb("code", [P, EC])
        vtmp = sb("vtmp", [P, EC])
        vtmp2 = sb("vtmp2", [P, EC])
        iota_i = sb("iota_i", [P, N], i32)
        iota = sb("iota", [P, N])
        ident = sb("ident", [P, P])
        ones = sb("ones", [P, N])
        eps_t = sb("eps_t", [P, 1])
        table = sb("table", [P, 1])
        stats = sb("stats", [N, 4, 4, 6])
        mv = sb("mv", [N, 4, 2])
        std = sb("std", [N, 4])
        rstd = sb("rstd", [N, 4])
        cnt = sb("cnt", [N, 2, N])
        deg = sb("deg", [N, 2])
        dsq = sb("dsq", [N, 2])
        dinv = sb("dinv", [N, 2])
        half_a = sb("half_a", [N, 2, N])
        a2t = sb("a2t", [N, N])
        a3t = sb("a3t", [N, N])
        a_s = sb("a_s", [N, N])
        a2_sum = sb("a2_sum", [N, 1])
        w96t = sb("w96t", [N, N])
        mask = sb("mask", [N, N])
        cls = sb("cls", [N, N])
        cls_i = sb("cls_i", [N, N], i32)
        mtmp = sb("mtmp", [N, N])
        nmx = sb("nmx", [N, H])
        sm = sb("sm", [N, H])
        rs = sb("rs", [N, H])
        u1t = sb("u1t", [N, N])
        hid = y_sb[:, 0:MID]

        ps = ctx.enter_context(nc.psum_tensor("ps", [P, 8, HALF], f32))

        def place(h):
            return 4 * (2 * (h // 8) + h % 2) + h % 8 // 2

        def y_ps(i):
            return ps[0:N, 2 * i:2 * i + 2, :]

        PARTS = [(0, MID, MID + HALF), (1, MID + HALF, D), (2, 0, MID)]
        SL = [slice(a, b) for _, a, b in PARTS]

        def part_ps(i):
            bank, a, b = PARTS[i]
            return ps[0:N, bank, 0:b - a]

        raw_in = [sem(f"raw_in{i}") for i in range(RAW_RING)]
        hi_done = sem("hi_done")
        lo_done = sem("lo_done")
        chunk_used = sem("chunk_used")
        consts = sem("consts")
        S = {}

        def ev(name):
            if name not in S:
                S[name] = sem(name)
            return S[name]

        y_slot = {"q": 0, "k": 1, "v": 0, "iq": 1, "ik": 0, "iv": 1}
        block = ctx.enter_context(nc.Block())

        def raw_slot(c):
            return c % RAW_RING

        def wait_raw(eng, c):
            eng.wait_ge(raw_in[raw_slot(c)], 16 * (c // RAW_RING + 1))

        def split_index(c):
            return SPLIT.index(c)

        def columns(tile):
            return slice(0, CW) if tile is None else slice(tile * D, (tile + 1) * D)

        tr_order = ["q", "k", "v", "iq", "ik"]
        bias_of = {"q": 0, "k": 1, "v": 2, "iq": 3, "ik": 4}
        NCONST = 5 + EC

        @block.sync
        def _(sp_):
            sp_.dma_start(xa[:], x).then_inc(ev("x_in"), 16)
            for c in range(NCHUNK):
                old = c - RAW_RING
                if old >= 0:
                    if old in WHOLE:
                        sp_.wait_ge(chunk_used, old + 1)
                    else:
                        sp_.wait_ge(lo_done, TPC * (split_index(old) + 1))
                sp_.dma_start(raw[:, raw_slot(c), :], weights[c]).then_inc(raw_in[raw_slot(c)], 16)
                if c == 25:
                    sp_.wait_ge(ev("tr_h"), 2)
                    sp_.dma_start(u[:], bias_rows[0:1, :].partition_broadcast(N)).then_inc(ev("bo_in"), 16)
                if c == 27:
                    sp_.wait_ge(ev("tr_ik"), 2)
                    sp_.dma_start(y_sb[:], bias_rows[1:2, :].partition_broadcast(N)).then_inc(ev("l1b_in"), 16)
                if c == 29:
                    sp_.wait_ge(ev("probs_tr"), 4)
                    sp_.dma_start(b_l2, bias_rows[2:3, :].partition_broadcast(N)).then_inc(ev("l2b_in"), 16)
                if c == 31:
                    sp_.wait_ge(ev("attn_mm"), 4)
                    sp_.dma_start(b2_tile, bias_rows[3:4, :].partition_broadcast(N)).then_inc(ev("b2_in"), 16)
            sp_.wait_ge(ev("result"), 2)
            sp_.dma_start(out[:, MID:D], xa[:, MID:D]).then_inc(ev("stored0"), 16)
            sp_.wait_ge(ev("stored0"), 16)

        @block.gpsimd
        def _(pool):
            pool.iota(iota_i[:], pattern=[[1, N]], base=0, channel_multiplier=0).then_inc(consts, 1)
            pool.memset(ident[:], 0.0).then_inc(consts, 1)
            pool.memset(later[:], 1.0).then_inc(consts, 1)
            pool.wait_ge(consts, 3)
            pool.affine_select(out=ident[:], in_=ident[:], compare_op=ALU.not_equal, fill=1.0, base=0,
                               pattern=[[-1, P]], channel_multiplier=1).then_inc(consts, 1)
            pool.affine_select(out=later[:], in_=later[:], compare_op=ALU.is_gt, fill=0.0, base=0,
                               pattern=[[1, P]], channel_multiplier=-1).then_inc(consts, 1)
            for c in range(EC):
                pool.memset(digit[:, c:c + 1], 16.0 ** c).then_inc(consts, 1)

            pool.wait_ge(ev("ecol_f"), 1)
            step = ev("code_step")
            steps = [0]

            def chained(ins):
                steps[0] += 1
                ins.then_inc(step, 1)
                pool.wait_ge(step, steps[0])

            for t in range(ETYPES + 1):
                k = (t - 1) % ETYPES
                dst = code if t == 0 else vtmp
                chained(pool.tensor_scalar(dst[:], ecol[:, 2, :], float(t), 2.0 ** k, ALU.is_equal, ALU.mult))
                if t:
                    chained(pool.tensor_tensor(code[:], code[:], vtmp[:], ALU.add))
            pool.wait_ge(consts, NCONST)
            chained(pool.tensor_tensor(code[:], code[:], digit[:], ALU.mult))

            pool.wait_ge(ev("ew_in"), 16)
            chained(pool.tensor_copy(ew_parts[:, 0, :], ew[:]))
            chained(pool.tensor_tensor(ew_rest[:, 0, :], ew[:], ew_parts[:, 0, :], ALU.subtract))
            chained(pool.tensor_copy(ew_parts[:, 1, :], ew_rest[:, 0, :]))
            chained(pool.tensor_tensor(ew_rest[:, 1, :], ew_rest[:, 0, :], ew_parts[:, 1, :], ALU.subtract))
            chained(pool.tensor_copy(ew_parts[:, 2, :], ew_rest[:, 1, :]))
            pool.wait_ge(ev("onehots"), 2)
            for i in range(3):
                pool.tensor_tensor(src_oh[:, :, 1 + i, :], src_oh[:, :, 0, :],
                                   ew_parts[:, i, :].unsqueeze(2).broadcast_to((P, EC, N)),
                                   ALU.mult).then_inc(ev("edge_rows"), 1)
            pool.wait_ge(ev("last"), 1)
            chained(pool.tensor_tensor(code[:], code[:], n_later[:], ALU.mult))
            pool.tensor_tensor(dst_oh[:, :, 1, :], dst_oh[:, :, 0, :],
                               code[:].unsqueeze(2).broadcast_to((P, EC, N)), ALU.mult).then_inc(ev("edge_rows"), 1)
            pool.wait_ge(ev("present"), 1)
            pool.wait_ge(ev("classes"), 1)
            chained(pool.tensor_copy(cls[:], cls_i[:]))
            chained(pool.tensor_scalar(mask[:], mask[:], 1.0, NEG, ALU.subtract, ALU.mult))
            pool.wait_ge(ev("softplus"), 1)
            for j in range(ETYPES):
                k = (j + 1) % ETYPES
                chained(pool.tensor_scalar(mtmp[:], cls[:], float(j), sp[0:N, k:k + 1], ALU.is_equal, ALU.mult))
                last = pool.tensor_tensor(mask[:], mask[:], mtmp[:], ALU.add)
                if j < ETYPES - 1:
                    chained(last)
            last.then_inc(ev("mask"), 1)
            for b in range(4):
                pool.wait_ge(ev("row_sum"), b + 1)
                pool.tensor_tensor(probs[:, 4 * b:4 * b + 4, :], probs[:, 4 * b:4 * b + 4, :],
                                   rs[:, 4 * b:4 * b + 4].unsqueeze(2).broadcast_to((N, 4, N)),
                                   ALU.mult).then_inc(ev("normalized"), 1)
            pool.wait_ge(ev("bo_in"), 16)
            pool.tensor_tensor(xa[:], xa[:], u[:], ALU.add).then_inc(ev("x_bo"), 1)
            pool.wait_ge(ev("l2b_in"), 16)
            pool.wait_ge(ev("a2_sum"), 1)
            pool.tensor_tensor(b_l2, b_l2, a2_sum[:].broadcast_to((N, D)), ALU.mult).then_inc(ev("l2b_rows"), 1)
            pool.wait_ge(ev("l1b_in"), 16)
            for i in range(2):
                pool.wait_ge(ev("stats1"), i + 1)
                pool.tensor_tensor(xa[:, SL[i]], xa[:, SL[i]], y_sb[:, SL[i]], ALU.add).then_inc(ev("x2_part"), 1)
            pool.wait_ge(ev("l2b_rows"), 1)
            pool.wait_ge(ev("x2"), 1)
            pool.tensor_tensor(xb[:], xa[:], b_l2, ALU.add).then_inc(ev("x2_b"), 1)
            pool.wait_ge(ev("b2_in"), 16)
            pool.wait_ge(ev("x3"), 1)
            pool.tensor_tensor(xa[:], xb[:], b2_tile, ALU.add).then_inc(ev("x3_b"), 1)

        @block.scalar
        def _(act):
            act.wait_ge(ev("eps"), 1)
            act.activation(table[:], eps_t[:], ACT.Sqrt).then_inc(ev("tables"), 1)
            act.dma_start(ecol_i[:], edge_cols).then_inc(ev("ecol_in"), 16)
            act.dma_start(erow_i[:], edge_rows).then_inc(ev("row_in"), 16)
            act.dma_start(tw[:], type_w).then_inc(ev("tw_in"), 16)
            act.dma_start(ew[:], edge_w).then_inc(ev("ew_in"), 16)
            act.dma_start(bt[:], bias_t).then_inc(ev("bt_in"), 16)
            act.dma_start(b1[:], b1_row).then_inc(ev("b1_in"), 16)

            def split(c, tile=None):
                if c in WHOLE:
                    return
                i = split_index(c)
                wait_raw(act, c)
                if i >= SPLIT_RING:
                    act.wait_ge(chunk_used, SPLIT[i - SPLIT_RING] + 1)
                s = columns(tile)
                act.activation(w_hi[:, i % SPLIT_RING, s], raw[:, raw_slot(c), s], ACT.Copy)\
                   .then_inc(hi_done, TPC if tile is None else 1)

            def evacuate(name):
                act.wait_ge(chunk_used, CPL * (LAYERS.index(name) + 1))
                i = tr_order.index(name)
                if i:
                    act.wait_ge(ev(f"tr_{tr_order[i - 1]}"), 2)
                for hf in range(2):
                    act.activation(y_sb[:, hf * HALF:(hf + 1) * HALF], y_ps(y_slot[name])[:, hf, :],
                                   ACT.Copy).then_inc(ev(f"y_{name}"), 1)

            def leading(name, src, per):
                for b in range(KT // per):
                    act.wait_ge(ev(f"{name}_t"), b + 1)
                    s = slice(per * b, per * b + per)
                    act.activation(parts_of[name][0][:, s, :], src[:, s, :], ACT.Copy).then_inc(ev(f"{name}_h"), 1)

            def leading_ps(name, tiles, per):
                for b in range(tiles // per):
                    act.wait_ge(ev(f"{name}_mm"), b + 1)
                    act.activation(parts_of[name][0][:, per * b:per * (b + 1), :],
                                   ps[:, 4 + b, 0:per * N].rearrange("p (k n) -> p k n", k=per),
                                   ACT.Copy).then_inc(ev(f"{name}_h"), 1)

            def root(i):
                act.wait_ge(ev(f"mv{i}"), 1)
                act.activation(std[:, i:i + 1], mv[:, i, 1:2], ACT.Sqrt, bias=eps_t[0:N, :]).then_inc(ev(f"std{i}"), 1)

            root(0)
            act.wait_ge(ev("row_in"), 16)
            act.activation(erow, erow_i[:], ACT.Copy).then_inc(ev("erow"), 1)
            act.wait_ge(ev("tr_h"), 2)
            act.wait_ge(ev("h_t"), 1)
            act.activation(h_t[:, 4:8, :], ps[:, 3, 0:4 * N].rearrange("p (k n) -> p k n", k=4),
                           ACT.Copy).then_inc(ev("h_t"), 1)
            leading("h", h_t, 4)
            act.wait_ge(ev("neg_abs"), 1)
            act.activation(spb[:], spa[:], ACT.Exp).then_inc(ev("sp_exp"), 1)
            act.wait_ge(ev("sp_exp"), 1)
            act.activation(sp[:], spb[:], ACT.Ln, bias=1.0).then_inc(ev("sp_ln"), 1)
            for c in range(3, 6):
                for tile in range(TPC):
                    split(c, tile)
            evacuate("q")
            for c in range(6, 8):
                for tile in range(TPC):
                    split(c, tile)
            split(8)
            leading("q", z_t, 4)
            split(9)
            evacuate("k")
            split(10)
            split(11)
            leading("k", z_t, 4)
            for c in range(12, 15):
                split(c)
            evacuate("v")
            split(15)
            split(16)
            act.wait_ge(ev("deg"), 2)
            act.activation(dsq[:], deg[:], ACT.Sqrt).then_inc(ev("dsq"), 1)
            act.wait_ge(chunk_used, 3 * CPL)
            leading("v", z_t, 4)
            split(17)
            split(18)
            evacuate("iq")
            for c in range(19, 22):
                split(c)
            evacuate("ik")
            act.wait_ge(ev("tables"), 1)
            act.activation(table[:], eps_t[:], ACT.Exp).then_inc(ev("tables"), 1)
            split(23)
            for b in range(4):
                if b == 2:
                    split(24)
                act.wait_ge(ev("row_max"), b + 1)
                for k in range(4):
                    h = 4 * b + k
                    last = act.activation(probs[:, h, :], probs[:, h, :], ACT.Exp, bias=nmx[:, h:h + 1], scale=-1.0,
                                          accum_out=sm[:, h:h + 1])
                last.then_inc(ev("exps"), 1)
            split(25, 0)
            for b in range(4):
                if b == 2:
                    split(25, 1)
                act.wait_ge(ev("probs_tr"), b + 1)
                act.activation(probs_t[:, 4 * b:4 * b + 4, :], ps[0:N, 4 + b, 0:4 * N].rearrange("p (h m) -> p h m", h=4),
                               ACT.Copy).then_inc(ev("probs_t"), 1)
            split(26, 0)
            leading("attn", z_t, 2)
            split(26, 1)
            split(27)
            split(28)
            act.wait_ge(ev("tables"), 2)
            act.activation(table[:], eps_t[:], ACT.Sqrt).then_inc(ev("tables"), 1)
            split(29)
            split(30)
            root(1)
            split(31)
            root(2)
            leading_ps("ah2", KT, 2)
            split(32)
            split(33)
            root(3)
            leading_ps("ah3", KT, 2)
            act.wait_ge(ev("hid_mm"), 1)
            for k in range(2):
                s = slice(k * P, (k + 1) * P)
                act.activation(hid[:, s], ps[0:N, 3, s], ACT.Relu).then_inc(ev("hid"), 1)
            leading_ps("ag", 2, 1)
            act.wait_ge(ev("result"), 3)
            act.dma_start(out[:, 0:MID], xa[:, 0:MID]).then_inc(ev("stored1"), 16)
            act.wait_ge(ev("stored1"), 16)

        @block.vector
        def _(dve):
            done = sem("dve_chain")
            chain = [0]

            def link(ins):
                chain[0] += 1
                ins.then_inc(done, 1)
                dve.wait_ge(done, chain[0])

            def split(c, tile=None):
                if c in WHOLE:
                    return
                i = split_index(c)
                dve.wait_ge(hi_done, TPC * i + (TPC if tile is None else tile + 1))
                s = columns(tile)
                dve.tensor_tensor(w_lo[:, i % SPLIT_RING, s], raw[:, raw_slot(c), s],
                                  w_hi[:, i % SPLIT_RING, s].bitcast(f32), ALU.subtract)\
                   .then_inc(lo_done, TPC if tile is None else 1)

            def add_bias(name, dst, banks):
                for b in range(2):
                    dve.wait_ge(ev(f"tr_{name}"), b + 1)
                    dve.tensor_tensor(dst[:, 4 * b:4 * b + 4, :],
                                      ps[:, banks[b], 0:4 * N].rearrange("p (k n) -> p k n", k=4),
                                      bt[:, bias_of[name], 4 * b:4 * b + 4].unsqueeze(2).broadcast_to((P, 4, N)),
                                      ALU.add).then_inc(ev(f"{name}_t"), 1)

            def rest(name, src, per, blocks):
                for b in blocks:
                    dve.wait_ge(ev(f"{name}_h"), b + 1)
                    s = slice(per * b, per * b + per)
                    hi, lo = parts_of[name]
                    dve.tensor_tensor(lo[:, s, :], src[:, s, :], hi[:, s, :].bitcast(f32),
                                      ALU.subtract).then_inc(ev(f"{name}_l"), 1)

            def rest_ps(name, tiles, per):
                for b in range(tiles // per):
                    s = slice(per * b, per * (b + 1))
                    hi, lo = parts_of[name]
                    dve.wait_ge(ev(f"{name}_h"), b + 1)
                    dve.tensor_tensor(lo[:, s, :], ps[:, 4 + b, 0:per * N].rearrange("p (k n) -> p k n", k=per),
                                      hi[:, s, :].bitcast(f32), ALU.subtract).then_inc(ev(f"{name}_l"), 1)

            def bn(i, seg, xt):
                return dve.bn_stats(stats[:, i, seg, :], xt)

            def aggregate(i, nseg):
                dve.bn_aggr(mv[:, i, :], stats[:, i, 0:nseg, :]).then_inc(ev(f"mv{i}"), 1)

            def reciprocal_std(i):
                dve.wait_ge(ev(f"std{i}"), 1)
                link(dve.reciprocal(rstd[:, i:i + 1], std[:, i:i + 1]))

            dve.memset(eps_t[:], EPS).then_inc(ev("eps"), 1)
            dve.memset(ones[:], 1.0).then_inc(ev("ones"), 1)
            link(dve.memset(coef[:], 1.0))
            dve.memset(coef[0:1, :], float(N)).then_inc(ev("coef"), 1)
            dve.wait_ge(ev("x_in"), 16)
            link(bn(0, 0, xa[:, 0:HALF]))
            link(bn(0, 1, xa[:, HALF:D]))
            aggregate(0, 2)
            dve.wait_ge(consts, 1)
            link(dve.tensor_copy(iota[:], iota_i[:]))
            dve.wait_ge(ev("mv0"), 1)
            for hf in range(2):
                s = slice(hf * HALF, (hf + 1) * HALF)
                if hf:
                    reciprocal_std(0)
                    dve.wait_ge(consts, 5)
                    dve.tensor_scalar(a_s[:], ident[0:N, 0:N], rstd[:, 0:1], None, ALU.mult).then_inc(ev("scale0"), 1)
                dve.tensor_scalar(u[:, s], xa[:, s], mv[:, 0, 0:1], 0.0, ALU.subtract, ALU.max).then_inc(ev("h0"), 1)
            dve.wait_ge(ev("ecol_in"), 16)
            dve.tensor_copy(ecol[:], ecol_i[:]).then_inc(ev("ecol_f"), 1)
            dve.wait_ge(ev("ecol_f"), 1)

            def one_hots(oh, k):
                dve.tensor_tensor(oh[:, :, 0, :], iota[:].unsqueeze(1).broadcast_to((P, EC, N)),
                                  ecol[:, k, :].unsqueeze(2).broadcast_to((P, EC, N)),
                                  ALU.is_equal).then_inc(ev("onehots"), 1)

            dve.wait_ge(ev("tr_h"), 1)
            dve.tensor_copy(h_t[:, 0:4, :], ps[:, 2, 0:4 * N].rearrange("p (k n) -> p k n", k=4)).then_inc(ev("h_t"), 1)
            one_hots(src_oh, 0)
            one_hots(dst_oh, 1)
            rest("h", h_t, 4, range(2))
            dve.wait_ge(ev("tw_in"), 16)
            link(dve.tensor_scalar(spa[:], tw[:], -1.0, None, ALU.mult))
            dve.tensor_tensor(spa[:], spa[:], tw[:], ALU.min).then_inc(ev("neg_abs"), 1)
            link(dve.tensor_scalar(vtmp2[:], ecol[:, 0, :], float(N), None, ALU.mult))
            link(dve.tensor_tensor(cell[:], vtmp2[:], ecol[:, 1, :], ALU.add))
            dve.wait_ge(ev("cells"), 1)
            dve.wait_ge(consts, NCONST)
            cells_ps = ps[:, 5:8, :].rearrange("p b n -> p (b n)")
            for c in range(EC):
                s = slice(P * c, P * c + P)
                dve.scalar_tensor_tensor(out=junk[:, s], in0=cells_ps[:, s], scalar=cell[:, c:c + 1], in1=later[:],
                                         op0=ALU.is_equal, op1=ALU.mult, accum_out=n_later[:, c:c + 1])\
                   .then_inc(ev("counted"), 1)
            dve.wait_ge(ev("counted"), EC)
            dve.tensor_scalar(n_later[:], n_later[:], 0.0, None, ALU.is_equal).then_inc(ev("last"), 1)
            for c in range(3, 8):
                for tile in range(TPC):
                    split(c, tile)
            dve.wait_ge(ev("bt_in"), 16)
            add_bias("q", z_t, (4, 7))
            split(8)
            rest("q", z_t, 4, range(2))
            split(9)
            split(10)
            dve.wait_ge(ev("graph_mm"), 2)
            dve.tensor_tensor(cnt[:, 0, :], ps[0:N, 5, 0:N], ident[0:N, 0:N], ALU.add).then_inc(ev("cnt0"), 1)
            link(dve.scalar_tensor_tensor(out=cls[:], in0=ident[0:N, 0:N], scalar=0.5, in1=ps[0:N, 5, N:2 * N],
                                          op0=ALU.mult, op1=ALU.max))
            dve.tensor_scalar(mask[:], cls[:], 0.0, None, ALU.is_gt).then_inc(ev("present"), 1)
            dve.tensor_scalar(cls_i[:], cls[:].bitcast(i32), 23, 3, ALU.logical_shift_right, ALU.bitwise_and)\
               .then_inc(ev("classes"), 1)
            dve.tensor_copy(w96t[:], ps[0:N, 6, 0:N]).then_inc(ev("w96t"), 1)
            dve.wait_ge(ev("cnt0"), 1)
            dve.tensor_reduce(deg[:, 0:1], cnt[:, 0, :], AX.X, ALU.add).then_inc(ev("deg"), 1)
            add_bias("k", z_t, (4, 7))
            split(11)
            rest("k", z_t, 4, range(2))
            split(12)
            split(13)
            split(14)
            dve.wait_ge(ev("cnt_tr"), 1)
            link(dve.tensor_copy(cnt[:, 1, :], ps[0:N, 5, 2 * N:3 * N]))
            dve.tensor_reduce(deg[:, 1:2], cnt[:, 1, :], AX.X, ALU.add).then_inc(ev("deg"), 1)
            add_bias("v", z_t, (4, 7))
            split(15)
            split(16)
            rest("v", z_t, 4, range(2))
            dve.wait_ge(ev("dsq"), 1)
            link(dve.reciprocal(dinv[:], dsq[:]))
            for i in range(2):
                dve.tensor_scalar(half_a[:, i, :], cnt[:, i, :], dinv[:, i:i + 1], None,
                                  ALU.mult).then_inc(ev("half_a"), 1)
            dve.wait_ge(ev("sp_ln"), 1)
            link(dve.tensor_scalar(spa[:], tw[:], 0.0, None, ALU.max))
            dve.tensor_tensor(sp[:], sp[:], spa[:], ALU.add).then_inc(ev("softplus"), 1)
            split(17)
            split(18)
            add_bias("iq", q2t, (4, 5))
            split(19)
            dve.wait_ge(ev("half_tr"), 2)
            dve.tensor_scalar(a2t[:], ps[0:N, 7, 0:N], dinv[:, 0:1], None, ALU.mult).then_inc(ev("adjacency"), 1)
            dve.tensor_scalar(a3t[:], ps[0:N, 7, N:2 * N], dinv[:, 1:2], None, ALU.mult).then_inc(ev("adjacency"), 1)
            split(20)
            split(21)
            add_bias("ik", k2t, (6, 7))
            dve.wait_ge(ev("mask"), 1)

            def row_maximum(b):
                s = slice(4 * b, 4 * b + 4)
                dve.wait_ge(ev("scores"), b + 1)
                link(dve.scalar_tensor_tensor(out=probs[:, s, :],
                                              in0=ps[0:N, 4 + b, 0:4 * N].rearrange("p (h m) -> p h m", h=4),
                                              scalar=-SCALE, in1=mask[:].unsqueeze(1).broadcast_to((N, 4, N)),
                                              op0=ALU.mult, op1=ALU.subtract))
                dve.tensor_reduce(nmx[:, s], probs[:, s, :], AX.X, ALU.min).then_inc(ev("row_max"), 1)

            def reciprocal_sum(b):
                s = slice(4 * b, 4 * b + 4)
                dve.wait_ge(ev("exps"), b + 1)
                dve.reciprocal(rs[:, s], sm[:, s]).then_inc(ev("row_sum"), 1)

            row_maximum(0)
            row_maximum(1)
            split(23)
            reciprocal_sum(0)
            reciprocal_sum(1)
            row_maximum(2)
            row_maximum(3)
            split(24)
            reciprocal_sum(2)
            reciprocal_sum(3)
            dve.wait_ge(ev("iv_half"), 1)
            dve.tensor_copy(v2[:, 0:HALF], y_ps(y_slot["iv"])[:, 0, :]).then_inc(ev("v2a"), 1)
            split(25, 0)

            dve.wait_ge(ev("iv_half"), 2)
            dve.tensor_copy(v2[:, HALF:D], y_ps(y_slot["iv"])[:, 1, :]).then_inc(ev("v2b"), 1)
            split(25, 1)
            for b in range(4):
                s = slice(2 * b, 2 * b + 2)
                dve.wait_ge(ev("attn_mm"), b + 1)
                dve.tensor_tensor(z_t[:, s, :], ps[:, 4 + b, 0:2 * N].rearrange("p (k n) -> p k n", k=2),
                                  bt[:, 5, s].unsqueeze(2).broadcast_to((P, 2, N)), ALU.add).then_inc(ev("attn_t"), 1)
                if b:
                    rest("attn", z_t, 2, [b - 1])
            rest("attn", z_t, 2, [3])
            split(26, 0)
            split(26, 1)
            split(27)
            dve.wait_ge(ev("row_mm"), 1)
            dve.tensor_copy(a2_sum[:], ps[0:N, 3, 0:1]).then_inc(ev("a2_sum"), 1)
            split(28)

            dve.wait_ge(ev("x_bo"), 1)
            for i in range(3):
                dve.wait_ge(ev("o_part"), i + 1)
                link(dve.tensor_tensor(xa[:, SL[i]], part_ps(i), xa[:, SL[i]], ALU.add))
                bn(1, i, xa[:, SL[i]]).then_inc(ev("stats1"), 1)
            dve.wait_ge(ev("stats1"), 3)
            aggregate(1, 3)
            dve.wait_ge(ev("mv1"), 1)
            dve.tensor_scalar(u[:, 0:N], xa[:, 0:N], mv[:, 1, 0:1], 0.0, ALU.subtract, ALU.max).then_inc(ev("u1"), 1)
            dve.wait_ge(ev("u1"), 1)
            dve.wait_ge(ev("l1b_in"), 16)
            link(dve.tensor_tensor(xa[:, SL[2]], xa[:, SL[2]], y_sb[:, SL[2]], ALU.add))
            for i in range(2):
                dve.wait_ge(ev("x2_part"), i + 1)
                bn(2, i, xa[:, SL[i]])
                if i == 0:
                    dve.wait_ge(ev("tr_u1"), 1)
                    dve.tensor_copy(u1t[:], ps[0:N, 4, 0:N]).then_inc(ev("u1t"), 1)
            reciprocal_std(1)
            dve.wait_ge(ev("l1_mm"), 1)
            dve.scalar_tensor_tensor(out=xa[:, 0:N], in0=ps[0:N, 5, 0:N], scalar=rstd[:, 1:2], in1=xa[:, 0:N],
                                     op0=ALU.mult, op1=ALU.add).then_inc(ev("x2"), 1)
            dve.wait_ge(ev("x2"), 1)
            link(bn(2, 2, xa[:, SL[2]]))

            def norm_and_scale(i, xt, at, key):
                aggregate(i, 3)
                dve.wait_ge(ev(f"mv{i}"), 1)
                for hf in range(2):
                    s = slice(hf * HALF, (hf + 1) * HALF)
                    if hf:
                        reciprocal_std(i)
                        dve.tensor_scalar(a_s[:], at[:], rstd[:, i:i + 1], None, ALU.mult).then_inc(ev(f"as_{key}"), 1)
                    dve.tensor_scalar(u[:, s], xt[:, s], mv[:, i, 0:1], 0.0, ALU.subtract, ALU.max)\
                       .then_inc(ev(f"u_{key}"), 1)

            norm_and_scale(2, xa[:], a2t, "ah2")
            split(29, 0)
            rest_ps("ah2", KT, 2)
            split(29, 1)
            for c in range(30, 33):
                split(c)
            dve.wait_ge(ev("x2_b"), 1)
            for i in range(3):
                dve.wait_ge(ev("W_part"), i + 1)
                x3 = dve.tensor_tensor(xb[:, SL[i]], part_ps(i), xb[:, SL[i]], ALU.add)
                if i == 2:
                    x3.then_inc(ev("x3"), 1)
                    dve.wait_ge(ev("x3"), 1)
                else:
                    link(x3)
                link(bn(3, i, xb[:, SL[i]]))
            norm_and_scale(3, xb, a3t, "ah3")
            rest_ps("ah3", KT, 2)
            split(33)
            rest_ps("ag", 2, 1)
            dve.wait_ge(ev("x3_b"), 1)
            for i in range(3):
                dve.wait_ge(ev("W2_part"), i + 1)
                dve.tensor_tensor(xa[:, SL[i]], part_ps(i), xa[:, SL[i]], ALU.add).then_inc(ev("result"), 1)

        @block.tensor
        def _(pe):
            def mm(o, l, r, start, stop):
                return pe.matmul(o, l, r, start=start, stop=stop)

            whole_of = {"h": h_t, "v": z_t, "attn": z_t}

            def wait_split(c, tile):
                if c not in WHOLE:
                    pe.wait_ge(lo_done, TPC * split_index(c) + tile + 1)

            def operands(c, z):
                if c in WHOLE:
                    wait_raw(pe, c)
                    return [(whole_of[z], raw[:, raw_slot(c), :].rearrange("p (t n) -> p t n", t=TPC))]
                i = split_index(c)
                hi = w_hi[:, i % SPLIT_RING, :].rearrange("p (t n) -> p t n", t=TPC)
                lo = w_lo[:, i % SPLIT_RING, :].rearrange("p (t n) -> p t n", t=TPC)
                zh, zl = parts_of[z]
                return [(zh, hi), (zh, lo), (zl, hi)]

            def chunk(name, c, z, tiles=range(TPC)):
                pairs = operands(c, z)
                for t in tiles:
                    wait_split(c, t)
                    kt = TPC * (c % CPL) + t
                    for pi, (zp, w) in enumerate(pairs):
                        for hf in range(2):
                            last = mm(y_ps(y_slot[name])[:, hf, :], zp[:, kt, :], w[:, t, hf * HALF:(hf + 1) * HALF],
                                      kt == 0 and pi == 0, kt == KT - 1 and pi == len(pairs) - 1)
                if TPC - 1 in tiles:
                    last.then_inc(chunk_used, 1)

            def last_chunks(chunks, kt0, z, outs, part_done, first=False, between=None,
                            z_ready=None):
                pairs = [operands(c, z) for c in chunks]
                for oi, (acc, a, b) in enumerate(outs):
                    for ci, c in enumerate(chunks):
                        for t in range(TPC):
                            if oi == 0:
                                wait_split(c, t)
                                if z_ready:
                                    pe.wait_ge(z_ready, t + 1)
                            kt = kt0 + TPC * ci + t
                            for pi, (zp, w) in enumerate(pairs[ci]):
                                stop = c == chunks[-1] and t == TPC - 1 and pi == len(pairs[ci]) - 1
                                last = mm(acc, zp[:, kt, :], w[:, t, a:b], first and ci == 0 and t == 0 and pi == 0, stop)
                        if oi == len(outs) - 1 and c != chunks[-1]:
                            last.then_inc(chunk_used, 1)
                    last.then_inc(part_done, 1)
                    if oi == 0 and between:
                        between()
                pe.wait_ge(part_done, len(outs))
                pe.nop().then_inc(chunk_used, 1)

            def transposes(name, banks):
                for b in range(2):
                    pe.wait_ge(ev(f"y_{name}"), b + 1)
                    for k in range(4):
                        kt = 4 * b + k
                        last = pe.transpose(ps[:, banks[b], k * N:(k + 1) * N], y_sb[:, kt * P:(kt + 1) * P],
                                            ident[0:N, 0:N])
                    last.then_inc(ev(f"tr_{name}"), 1)

            def keep_busy(n):
                for _ in range(n):
                    mm(ps[:, 6, 0:P], ident[:], ident[:], True, True)

            pe.wait_ge(consts, 5)
            keep_busy(WARM_UP)
            pe.wait_ge(ev("scale0"), 1)
            for b in range(2):
                pe.wait_ge(ev("h0"), b + 1)
                for k in range(4):
                    kt = 4 * b + k
                    last = mm(ps[:, 2 + b, k * N:(k + 1) * N], u[:, kt * P:(kt + 1) * P], a_s[:], True, True)
                last.then_inc(ev("tr_h"), 1)

            pe.wait_ge(ev("h_t"), 1)
            chunk("q", 0, "h", (0,))
            pe.wait_ge(ev("coef"), 1)
            pe.wait_ge(ev("erow"), 1)
            for b in range(3):
                last = mm(ps[:, 5 + b, :], coef[:], erow[:, b * HALF:(b + 1) * HALF], True, True)
            last.then_inc(ev("cells"), 1)
            chunk("q", 0, "h", (1,))
            pe.wait_ge(ev("h_t"), 2)
            pe.wait_ge(ev("h_l"), 2)
            for c in range(1, 4):
                chunk("q", c, "h")
            chunk("k", 4, "h")
            transposes("q", (4, 7))
            for c in range(5, 8):
                chunk("k", c, "h")
            pe.wait_ge(ev("edge_rows"), 4)
            for c in range(EC):
                last = mm(ps[0:N, 5, 0:2 * N], src_oh[:, c, 0, :], dst_oh[:, c, :, :].rearrange("p a n -> p (a n)"),
                          c == 0, c == EC - 1)
            last.then_inc(ev("graph_mm"), 1)
            for c in range(EC):
                for i in range(3):
                    last = mm(ps[0:N, 6, 0:N], dst_oh[:, c, 0, :], src_oh[:, c, 1 + i, :],
                              c == 0 and i == 0, c == EC - 1 and i == 2)
            last.then_inc(ev("graph_mm"), 1)
            pe.wait_ge(ev("y_q"), 2)
            chunk("v", 8, "h")
            pe.wait_ge(ev("q_t"), 2)
            transposes("k", (4, 7))
            for c in range(9, 12):
                chunk("v", c, "h")
            pe.wait_ge(ev("q_l"), 2)
            pe.wait_ge(ev("y_k"), 2)
            chunk("iq", 12, "q")
            pe.wait_ge(ev("cnt0"), 1)
            pe.transpose(ps[0:N, 5, 2 * N:3 * N], cnt[:, 0, :], ident[0:N, 0:N]).then_inc(ev("cnt_tr"), 1)
            pe.wait_ge(ev("k_t"), 2)
            transposes("v", (4, 7))
            for c in range(13, 16):
                chunk("iq", c, "q")
            pe.wait_ge(ev("k_l"), 2)
            pe.wait_ge(ev("y_v"), 2)
            chunk("ik", 16, "k")
            pe.wait_ge(ev("v_t"), 2)
            pe.wait_ge(ev("deg"), 2)
            transposes("iq", (4, 5))
            chunk("ik", 17, "k")
            pe.wait_ge(ev("half_a"), 2)
            for i in range(2):
                pe.transpose(ps[0:N, 7, i * N:(i + 1) * N], half_a[:, i, :], ident[0:N, 0:N]).then_inc(ev("half_tr"), 1)
            for c in range(18, 20):
                chunk("ik", c, "k")
            pe.wait_ge(ev("v_l"), 2)
            pe.wait_ge(ev("y_iq"), 2)
            chunk("iv", 20, "v", (0,))
            pe.wait_ge(ev("w96t"), 1)
            pe.wait_ge(ev("adjacency"), 2)
            transposes("ik", (6, 7))
            chunk("iv", 20, "v", (1,))
            pe.wait_ge(ev("iq_t"), 2)
            pe.wait_ge(ev("ik_t"), 2)
            for pair in range(2):
                for k in range(4):
                    for odd in range(2):
                        kt = 4 * pair + k
                        r = slice(DH * odd, DH * odd + DH)
                        last = mm(ps[0:N, 4 + 2 * pair + odd, k * N:(k + 1) * N], q2t[r, kt, :], k2t[r, kt, :], True, True)
                        if k == 3:
                            last.then_inc(ev("scores"), 1)
            chunk("iv", 21, "v")

            def transpose_probs(banks):
                for b in banks:
                    pe.wait_ge(ev("normalized"), b + 1)
                    for k in range(4):
                        last = pe.transpose(ps[0:N, 4 + b, k * N:(k + 1) * N], probs[:, 4 * b + k, :], ident[0:N, 0:N])
                    last.then_inc(ev("probs_tr"), 1)

            last_chunks([22, 23], 4, "v", [(y_ps(1)[:, hf, :], hf * HALF, (hf + 1) * HALF) for hf in range(2)],
                        ev("iv_half"), between=lambda: transpose_probs(range(2)))
            transpose_probs(range(2, 4))
            for b in range(4):
                pe.wait_ge(ev("v2b" if b >= 2 else "v2a"), 1)
                pe.wait_ge(ev("probs_t"), 2 * (b // 2) + 2)
                for k in range(4):
                    h = 4 * b + k
                    r = slice(DH * (h % 2), DH * (h % 2) + DH)
                    c0 = (k // 2) * N
                    last = mm(ps[r, 4 + b, c0:c0 + N], v2[:, h * DH:(h + 1) * DH], probs_t[:, place(h), :], True, True)
                last.then_inc(ev("attn_mm"), 1)

            def residual_layer(c0, z, blocks, part_done):
                for ci in range(CPL - 2):
                    pe.wait_ge(blocks, ci + 1)
                    pairs = operands(c0 + ci, z)
                    for t in range(TPC):
                        wait_split(c0 + ci, t)
                        kt = TPC * ci + t
                        for pi, (zp, w) in enumerate(pairs):
                            for i, (_, a, b) in enumerate(PARTS):
                                last = mm(part_ps(i), zp[:, kt, :], w[:, t, a:b], kt == 0 and pi == 0, False)
                    last.then_inc(chunk_used, 1)
                pe.wait_ge(blocks, CPL)
                last_chunks([c0 + 2, c0 + 3], 4, z, [(part_ps(i), a, b) for i, (_, a, b) in enumerate(PARTS)], part_done)

            pe.wait_ge(ev("ones"), 1)
            mm(ps[0:N, 3, 0:1], a2t[:], ones[0:N, 0:1], True, True).then_inc(ev("row_mm"), 1)
            residual_layer(6 * CPL, "attn", ev("attn_l"), ev("o_part"))
            keep_busy(KEEP_BUSY[0])
            pe.wait_ge(ev("u1"), 1)
            pe.transpose(ps[0:N, 4, 0:N], u[:, 0:N], ident[0:N, 0:N]).then_inc(ev("tr_u1"), 1)
            pe.wait_ge(ev("u1t"), 1)
            mm(ps[0:N, 5, 0:N], u1t[:], w96t[:], True, True).then_inc(ev("l1_mm"), 1)
            keep_busy(KEEP_BUSY[1])

            def aggregation(key):
                pe.wait_ge(ev(f"as_{key}"), 1)
                for b in range(4):
                    pe.wait_ge(ev(f"u_{key}"), b // 2 + 1)
                    for k in range(2):
                        kt = 2 * b + k
                        last = mm(ps[:, 4 + b, k * N:(k + 1) * N], u[:, kt * P:(kt + 1) * P], a_s[:], True, True)
                    last.then_inc(ev(f"{key}_mm"), 1)

            aggregation("ah2")
            residual_layer(7 * CPL, "ah2", ev("ah2_l"), ev("W_part"))
            pe.wait_ge(ev("b1_in"), 16)
            mm(ps[0:N, 3, 0:MID], ones[0:1, :], b1[:], True, False)
            keep_busy(KEEP_BUSY[2])
            aggregation("ah3")
            i = split_index(C_W1)
            hi_z, lo_z = parts_of["ah3"]
            for kt in range(KT):
                if kt % 4 == 0:
                    wait_split(C_W1, kt // 4)
                if kt % 2 == 0:
                    pe.wait_ge(ev("ah3_l"), kt // 2 + 1)
                s = slice(kt * MID, (kt + 1) * MID)
                hi, lo = w_hi[:, i % SPLIT_RING, s], w_lo[:, i % SPLIT_RING, s]
                mm(ps[0:N, 3, 0:MID], hi_z[:, kt, :], hi, False, False)
                mm(ps[0:N, 3, 0:MID], hi_z[:, kt, :], lo, False, False)
                last = mm(ps[0:N, 3, 0:MID], lo_z[:, kt, :], hi, False, kt == KT - 1)
            last.then_inc(ev("hid_mm"), 1)
            for k in range(2):
                pe.wait_ge(ev("hid"), k + 1)
                mm(ps[:, 4 + k, 0:N], hid[:, k * P:(k + 1) * P], a3t[:], True, True).then_inc(ev("ag_mm"), 1)
            last_chunks([C_W2], 0, "ag", [(part_ps(i), a, b) for i, (_, a, b) in enumerate(PARTS)], ev("W2_part"),
                        first=True, z_ready=ev("ag_l"))


def kernel(**inputs):
    import numpy as np
    import concourse.bacc as bacc
    from concourse.bass_utils import run_bass_kernel_spmd

    a = {k: np.asarray(v) for k, v in inputs.items()}

    def chunks(w_kn):
        k, n = w_kn.shape
        return w_kn.reshape(k // (TPC * P), TPC, P, n).transpose(0, 2, 1, 3).reshape(-1, P, TPC * n)

    full = ["L0_gnn_wq", "L0_gnn_wk", "L0_gnn_wv", "L0_gnn_wiq", "L0_gnn_wik", "L0_gnn_wiv", "L0_gnn_wo", "L2_gnn_W"]
    w1 = a["L3_gnn_W1"].reshape(KT, P, MID).transpose(1, 0, 2).reshape(1, P, CW)
    weights = np.ascontiguousarray(np.concatenate([chunks(a[n].T) for n in full] + [w1, chunks(a["L3_gnn_W2"])]))
    cols = ["L0_gnn_bq", "L0_gnn_bk", "L0_gnn_bv", "L0_gnn_biq", "L0_gnn_bik", "L0_gnn_biv"]
    bias_t = np.ascontiguousarray(np.stack([a[n].reshape(KT, P).T for n in cols], axis=1))
    bias_rows = np.stack([a[n] for n in ("L0_gnn_bo", "L1_gnn_bias", "L2_gnn_b", "L3_gnn_b2")])
    edge_cols = np.ascontiguousarray(np.stack([a[n].reshape(EC, P).T for n in ("src", "dst", "edge_type_5")], axis=1))
    arrays = {
        "x": a["x"], "weights": weights, "bias_t": bias_t, "bias_rows": bias_rows,
        "b1_row": a["L3_gnn_b1"].reshape(1, MID), "edge_cols": edge_cols,
        "edge_w": np.ascontiguousarray(a["edge_weight"].reshape(EC, P).T),
        "edge_rows": np.ascontiguousarray(np.stack([a["src"], a["dst"]])),
        "type_w": np.ascontiguousarray(np.broadcast_to(a["L0_gnn_edge_type_weights"], (P, ETYPES))),
    }
    nc = bacc.Bacc("TRN2", target_bir_lowering=False, num_devices=1)
    aps = [nc.dram_tensor(n, v.shape, mybir.dt.from_np(v.dtype), kind="ExternalInput").ap() for n, v in arrays.items()]
    out = nc.dram_tensor("out", (N, D), mybir.dt.float32, kind="ExternalOutput").ap()
    gnn_kernel(nc, *aps, out)
    r = run_bass_kernel_spmd(nc, [arrays], core_ids=[0])
    return r.results[0]["out"]
```
